# Optimizing a Trainium2 kernel written in Bass

```python
import numpy as np
import jax
import jax.numpy as jnp

def _softmax(x, axis=-1):
    return jax.nn.softmax(x, axis=axis)
def _gelu(x):
    return jax.nn.gelu(x, approximate=True)
def _silu(x):
    return jax.nn.silu(x)
def _sigmoid(x):
    return jax.nn.sigmoid(x)
def _layernorm(x, axis=-1, eps=1e-5):
    m = jnp.mean(x, axis=axis, keepdims=True)
    v = jnp.var(x, axis=axis, keepdims=True)
    return (x - m) / jnp.sqrt(v + eps)
def _scatter_add(tgt, idx, src, axis=0):
    return tgt.at[idx].add(src)
def _segment_sum(src, seg, n):
    return jax.ops.segment_sum(src, seg, n)

kernel_name = 'mk_metaformer_d1_conv_nchw128_348d61'

def setup_inputs(seed: int = 0):
    np.random.seed(seed)
    _w = jnp.asarray
    def _rec_inputs():
        import jax
        import jax.numpy as jnp
        _gk = jax.random.key(seed)
        x = -0.000125 + 0.9999 * jax.random.normal(jax.random.fold_in(_gk, 1), (16, 128, 128, 128), jnp.float32)
        return x
    x = _rec_inputs()
    def _L0_conv_setup():
        import jax, jax.numpy as jnp
        import numpy as np
        HEADS = 4
        DIM_HEAD = 32
        DIM = 128
        HIDDEN = HEADS * DIM_HEAD
        key = jax.random.key(seed)
        k1, k2, k3, k4 = jax.random.split(key, 4)
        b, c, h, w = (16, DIM, 128, 128)
        x = jax.random.normal(k1, (b, c, h, w), dtype=jnp.float32)
        w_qkv = jax.random.normal(k2, (HIDDEN * 3, DIM), dtype=jnp.float32) * (1.0 / np.sqrt(DIM))
        w_out = jax.random.normal(k3, (DIM, HIDDEN), dtype=jnp.float32) * (1.0 / np.sqrt(HIDDEN))
        b_out = jax.random.normal(k4, (DIM,), dtype=jnp.float32) * 0.01
        g = jnp.ones((DIM,), dtype=jnp.float32)
        return {'x': x, 'w_qkv': w_qkv, 'w_out': w_out, 'b_out': b_out, 'g': g}
    _L0_conv_all = _L0_conv_setup()
    _L0_conv_in = {k: v for k, v in _L0_conv_all.items() if k in ('w_qkv', 'w_out', 'b_out', 'g', )}
    del _L0_conv_all

    def _L0_ffn_setup():
        import jax, jax.numpy as jnp
        import numpy as np
        BN_EPS = 1e-05
        key = jax.random.key(seed)
        k1, k2, k3 = jax.random.split(key, 3)
        B, T, I, H = (64, 2048, 128, 128)
        x = jax.random.normal(k1, (B, T, I), dtype=jnp.float32)
        W = jax.random.normal(k2, (H, I), dtype=jnp.float32) * (1.0 / np.sqrt(I))
        V = jnp.linalg.qr(jax.random.normal(k3, (H, H), dtype=jnp.float32))[0]
        gamma = jnp.ones((H,), dtype=jnp.float32)
        beta = jnp.zeros((H,), dtype=jnp.float32)
        return {'x': x, 'W': W, 'V': V, 'gamma': gamma, 'beta': beta}
    _L0_ffn_all = _L0_ffn_setup()
    _L0_ffn_in = {k: v for k, v in _L0_ffn_all.items() if k in ('W', 'V', 'gamma', 'beta', )}
    del _L0_ffn_all

    return {
        "x": x,
        "L0_conv_w_qkv": _L0_conv_in["w_qkv"],
        "L0_conv_w_out": _L0_conv_in["w_out"],
        "L0_conv_b_out": _L0_conv_in["b_out"],
        "L0_conv_g": _L0_conv_in["g"],
        "L0_ffn_W": _L0_ffn_in["W"],
        "L0_ffn_V": _L0_ffn_in["V"],
        "L0_ffn_gamma": _L0_ffn_in["gamma"],
        "L0_ffn_beta": _L0_ffn_in["beta"],
    }

def reference(x, L0_conv_w_qkv, L0_conv_w_out, L0_conv_b_out, L0_conv_g, L0_ffn_W, L0_ffn_V, L0_ffn_gamma, L0_ffn_beta):
    import jax
    import jax.numpy as jnp
    def _L0_conv_ref(x, w_qkv, w_out, b_out, g):
        import jax, jax.numpy as jnp
        import numpy as np
        HEADS = 4
        DIM_HEAD = 32
        DIM = 128
        HIDDEN = HEADS * DIM_HEAD
        b, c, h, w = x.shape
        n = h * w
        scale = DIM_HEAD ** (-0.5)
        qkv = jnp.einsum('bcxy,oc->boxy', x, w_qkv)
        q, k, v = jnp.split(qkv, 3, axis=1)
        rs = lambda t: t.reshape(b, HEADS, DIM_HEAD, n)
        q, k, v = (rs(q), rs(k), rs(v))
        q = jax.nn.softmax(q, axis=-2) * scale
        k = jax.nn.softmax(k, axis=-1)
        v = v / n
        context = jnp.einsum('bhdn,bhen->bhde', k, v)
        out = jnp.einsum('bhde,bhdn->bhen', context, q)
        out = out.reshape(b, HIDDEN, h, w)
        out = jnp.einsum('bcxy,oc->boxy', out, w_out) + b_out[None, :, None, None]
        mean = jnp.mean(out, axis=1, keepdims=True)
        var = jnp.var(out, axis=1, keepdims=True)
        return (out - mean) * jax.lax.rsqrt(var + 1e-05) * g[None, :, None, None]

    def _L0_ffn_ref(x, W, V, gamma, beta):
        import jax, jax.numpy as jnp
        import numpy as np
        BN_EPS = 1e-05
        B, T, H = (x.shape[0], x.shape[1], W.shape[0])
        Wx = jnp.einsum('bti,hi->bth', x, W)
        flat = Wx.reshape(B * T, H)
        mean = jnp.mean(flat, axis=0)
        var = jnp.var(flat, axis=0)
        Wx = ((flat - mean) * jax.lax.rsqrt(var + BN_EPS) * gamma + beta).reshape(B, T, H)
        Vt = V.T

        def step(yt, wx_t):
            yt = jax.nn.sigmoid(wx_t + yt @ Vt)
            return (yt, yt)
        y0 = jnp.zeros((B, H), dtype=Wx.dtype)
        _, ys = jax.lax.scan(step, y0, jnp.swapaxes(Wx, 0, 1))
        return jnp.swapaxes(ys, 0, 1)

    def _gn(v, G=32, eps=1e-5):
        B_, C_, H_, W_ = v.shape
        g = v.reshape(B_, G, C_ // G, H_, W_)
        m = jnp.mean(g, axis=(2, 3, 4), keepdims=True)
        s = jnp.var(g, axis=(2, 3, 4), keepdims=True)
        return ((g - m) / jnp.sqrt(s + eps)).reshape(v.shape)

    def _ln_c(v, eps=1e-6):
        m = jnp.mean(v, axis=1, keepdims=True)
        s = jnp.var(v, axis=1, keepdims=True)
        return (v - m) / jnp.sqrt(s + eps)

    def _ln_t(v, eps=1e-5):
        m = jnp.mean(v, axis=-1, keepdims=True)
        s = jnp.var(v, axis=-1, keepdims=True)
        return (v - m) / jnp.sqrt(s + eps)

    def _to_tokens(v):
        B_, C_, H_, W_ = v.shape
        return v.reshape(B_, C_, H_ * W_).transpose(0, 2, 1)
    def _from_tokens(t, like):
        B_, C_, H_, W_ = like.shape
        return t.transpose(0, 2, 1).reshape(B_, C_, H_, W_)

    x = x + _L0_conv_ref(_ln_c(x), L0_conv_w_qkv, L0_conv_w_out, L0_conv_b_out, L0_conv_g)
    t = _to_tokens(x)
    t = t + _L0_ffn_ref(_ln_t(t), L0_ffn_W, L0_ffn_V, L0_ffn_gamma, L0_ffn_beta)
    x = _from_tokens(t, x)
    return x


_drawn_inputs = setup_inputs


def setup_inputs(seed=0):
    import zlib

    import numpy as np

    out = dict(_drawn_inputs(seed))
    spreads = {'L0_conv_g': (1.0, 0.2), 'L0_ffn_gamma': (1.0, 0.6), 'L0_ffn_beta': (0.0, 0.556)}
    factors = {'L0_conv_w_qkv': 8.0, 'L0_conv_w_out': 8.0}
    for name, (base, spread) in spreads.items():
        noise = np.random.default_rng([zlib.crc32(name.encode()), seed]).standard_normal(out[name].shape)
        drawn = base * np.exp(spread * noise) if base else spread * noise
        out[name] = jnp.asarray(drawn.astype(out[name].dtype))
    for name, factor in factors.items():
        out[name] = (out[name] * factor).astype(out[name].dtype)
    return out
```

```python
import numpy as np
import concourse.bass as bass
from concourse import mybir
from contextlib import ExitStack

F32 = mybir.dt.float32
I32 = mybir.dt.int32
ALU = mybir.AluOpType
ACT = mybir.ActivationFunctionType
AX = mybir.AxisListType.X

C = 128
HEADS = 4
DH = C // HEADS
CH = 512
TL = CH // 128
SEG = 1024
T = 64
TH = T // 2
GS = 4
NG = T // GS
RING = 2
CONTRACT = 1.01


def build(nc, x, w_qkv, w_out, b_out, g, W, V, gamma, beta, out):
    B, _, N = x.shape
    NC = N // CH
    J = N // SEG
    NB = SEG // T
    COLS = B * J
    CC = COLS // 2
    TOK = B * N
    assert NC % 2 == 0 and NC >= 8 and NB % 2 == 0 and CC * GS <= 512 and RING * GS <= T

    x1_s = nc.dram_tensor("x1_scratch", (NB, C, COLS, T), F32).ap()
    th_s = nc.dram_tensor("th_scratch", (2 * NB, C, COLS, TH), F32).ap()

    with ExitStack() as ctx:
        def sem(name):
            return ctx.enter_context(nc.semaphore(name))

        def sb(name, shape, dt=F32, stack=ctx):
            return stack.enter_context(nc.sbuf_tensor(name, shape, dt))

        bank = [ctx.enter_context(nc.psum_tensor(f"bank{i}", [C, 512], F32)) for i in range(8)]

        ident = sb("ident", [C, C])
        VT = sb("VT", [C, C])
        WzT = sb("WzT", [C, C])
        zbias = sb("zbias", [C, 1])
        y = [sb(f"y{c}", [C, RING, GS, CC]) for c in range(2)]
        y_start = [sb(f"y_start{c}", [C, CC]) for c in range(2)]
        n_sweeps = sb("n_sweeps", [1, 1], I32)

        w_in, ident_ok = sem("w_in"), sem("ident_ok")
        wT_ps, cert = sem("wT_ps"), sem("cert")
        wT_sb, setup, setup_pool, dve_chain = (sem(s) for s in ("wT_sb", "setup", "setup_pool", "dve_chain"))
        settled = {e.engine: sem(f"settled_{n}") for n, e in (("sp", nc.sync), ("pool", nc.gpsimd), ("dve", nc.vector))}
        x_var, o_var, s_var, bn_veps = (sem(s) for s in ("x_var", "o_var", "s_var", "bn_veps"))
        x_bn, x_mv, x_rstd, x_mr, kc_max, z_upd, q_max, q_tot, img_init, img_rz = (
            sem(s) for s in ("x_bn", "x_mv", "x_rstd", "x_mr", "kc_max", "z_upd", "q_max", "q_tot", "img_init", "img_rz"))
        o_bn, o_mv, o_rstd, s_bn, s_mv, s_rstd = (
            sem(s) for s in ("o_bn", "o_mv", "o_rstd", "s_bn", "s_mv", "s_rstd"))
        x_in = [sem(f"x_in{p}") for p in range(2)]
        xT_ps, stat, ln = sem("xT_ps"), sem("stat"), sem("ln")
        xh_ps, xh_sb = sem("xh_ps"), sem("xh_sb")
        k_ps, k_max, ek_sb, q_ps, q_sub, q_exp, q_rec, q_nrm = (
            sem(s) for s in ("k_ps", "k_max", "ek_sb", "q_ps", "q_sub", "q_exp", "q_rec", "q_nrm"))
        qh_ps, qh_sb, ekT_ps, ekT_sb, g_ps, g_upd = (
            sem(s) for s in ("qh_ps", "qh_sb", "ekT_ps", "ekT_sb", "g_ps", "g_upd"))
        q_kept = [sem(f"q_kept{p}") for p in range(2)]
        gs_sb, gT_ps, gT_sb, ctx_ps, ctx_sb, m_ps, m_sb = (
            sem(s) for s in ("gs_sb", "gT_ps", "gT_sb", "ctx_ps", "ctx_sb", "m_ps", "m_sb"))
        x2_in = [sem(f"x2_in{p}") for p in range(2)]
        q_in = [sem(f"q_in{p}") for p in range(2)]
        x2T_ps, x2T_sb, o_ps, x1T_sb, thT_sb = (
            sem(s) for s in ("x2T_ps", "x2T_sb", "o_ps", "x1T_sb", "thT_sb"))
        x1_ps, th_ps, gram_ps, x1_sb, th_sb = (
            sem(s) for s in ("x1_ps", "th_ps", "gram_ps", "x1_sb", "th_sb"))
        x1_st = [sem(f"x1_st{p}") for p in range(2)]
        th_st = [sem(f"th_st{p}") for p in range(2)]
        bn_c, bn_ps, bn_var, bn_rstd, bn_w, bn_wps, bn_done = (
            sem(s) for s in ("bn_c", "bn_ps", "bn_var", "bn_rstd", "bn_w", "bn_wps", "bn_done"))
        th_in = [sem(f"th_in{h}") for h in range(2)]
        x1_in = [sem(f"x1_in{p}") for p in range(2)]
        out_st = [sem(f"out_st{p}") for p in range(2)]
        start_ok = [sem(f"start_ok{c}") for c in range(2)]
        z_done = sem("z_done")
        pre_ps = [sem(f"pre_ps{c}") for c in range(2)]
        y_sb = [sem(f"y_sb{c}") for c in range(2)]
        slot_free = [sem(f"slot_free{c}") for c in range(2)]

        a = ExitStack()

        def sa(name, shape, dt=F32):
            return sb(name, shape, dt, a)

        wqkv_in = sa("wqkv_in", [C, 3, C])
        wout_in = sa("wout_in", [C, C])
        W_in = sa("W_in", [C, C])
        V_in = sa("V_in", [C, C])
        cols_in = sa("cols_in", [C, 2])
        gb = sa("gb", [C, 2, C])
        WqT, WkT, WvT = sa("WqT", [C, C]), sa("WkT", [C, C]), sa("WvT", [C, C])
        WoT = sa("WoT", [C, 2, C])
        bias_rows = sa("bias_rows", [C, 2, C])
        WT = sa("WT", [C, C])
        head_mask = sa("head_mask", [C, C])
        tmp = sa("tmp", [C, C])
        small = sa("small", [C, 16])
        cert_row = sa("cert_row", [1, 4])
        minus_half = sa("minus_half", [C, TL])
        veps = sa("veps", [C, 3, TL])
        zeros = sa("zeros", [C, C + 1])

        xin = sa("xin", [C, 2, CH])
        bn6 = sa("bn6", [C, 2, TL, 6])
        mv = sa("mv", [C, 2, TL, 2])
        rstd = sa("rstd", [C, 2, TL])
        nmr = sa("nmr", [C, 2, TL])
        xhT = sa("xhT", [C, 2, TL, C])
        xh = sa("xh", [C, 2, CH])
        nmax = sa("nmax", [C, 2])
        ncmax = sa("ncmax", [C, 1])
        alpha = sa("alpha", [C, 2])
        zc = sa("zc", [C, 2])
        Z = sa("Z", [C, 1])
        G = sa("G", [C, C])
        Gs = sa("Gs", [C, C])
        GT = sa("GT", [C, C])
        ctxT = sa("ctxT", [C, C])
        MT = sa("MT", [C, 2, C])
        ek = sa("ek", [C, 2, CH])
        ekT = sa("ekT", [C, 2, CH])
        q_mx = sa("q_mx", [C, TL * HEADS])
        qs = sa("qs", [C, 2, CH])
        q_sum = sa("q_sum", [C, TL * HEADS])
        q_inv = sa("q_inv", [C, 2, TL * HEADS])
        qhT = sa("qhT", [C, 2, CH])
        qh = sa("qh", [C, 2, CH])
        q_image = sa("q_image", [C, N])

        x2in = sa("x2in", [C, 2, CH])
        qin = sa("qin", [C, 2, CH])
        x2T = sa("x2T", [C, 2, CH])
        o6 = sa("o6", [C, TL, 6])
        omv = sa("omv", [C, TL, 2])
        orstd = sa("orstd", [C, TL])
        x1T = sa("x1T", [C, 2, TL, C])
        s6 = sa("s6", [C, TL, 6])
        smv = sa("smv", [C, TL, 2])
        srstd = sa("srstd", [C, TL])
        thT = sa("thT", [C, 2, TL, C + 1])
        x1o = sa("x1o", [C, 2, CH])
        tho = sa("tho", [C, 2, CH])
        cov = sa("cov", [C, C + 1])
        Wz = sa("Wz", [C, C])

        gram = bank[0]
        xT_b = [bank[1], bank[2]]
        xh_b, k_b, q_b, tr_b, g_b = bank[3], bank[4], bank[5], bank[6], bank[7]
        x2T_b, o_b, x1_b, th_b = bank[1], [bank[2], bank[3]], bank[4], bank[5]

        def settle(eng):
            eng.sem_inc(settled[eng.engine], 1)

        def steps(eng, b, emit, first, inner, last):
            def one(s, k=None):
                n = b * NC + s if k is None else b * NC + 2 * k + s

                def cnt(d):
                    c = b * (NC // 2) + (s + d) // 2 + 1
                    return c if k is None else c + k
                local = s if k is None else 2 * k + s
                emit(n, s % 2, lambda d: k is not None or 0 <= s + d < NC, cnt, local)
            for s in range(first, inner):
                one(s)
            with eng.Fori(0, (NC - 1 - last - inner) // 2) as k:
                one(inner, k)
                one(inner + 1, k)
            for s in range(NC - 1 - last, NC - 1 + 1 + last2(first)):
                one(s)

        def last2(first):
            return 3 if first < 0 else 1

        def a1_steps(eng, b, emit):
            steps(eng, b, emit, -1, 4, 1)

        def a2_steps(eng, b, emit):
            steps(eng, b, emit, 0, 2, 1)

        a.close()
        th_t = [sb(f"th_t{h}", [C, COLS, TH]) for h in range(2)]
        x1_t = [sb(f"x1_t{p}", [C, COLS, T]) for p in range(2)]
        z_b = [[bank[1], bank[2]], [bank[3], bank[4]]]
        out_v = out.rearrange("b c (j k t) -> k c b j t", k=NB, t=T)
        SWEEP = NB * NG
        zero_col = [yb[:].rearrange("p (b j) -> p b j", j=J) for yb in y_start]

        def scan_dma(sp):
            sp.wait_ge(bn_done, 1)
            sp.dma_start(th_t[0][:], th_s[2 * NB - 2]).then_inc(th_in[0], 16)
            sp.dma_start(th_t[1][:], th_s[2 * NB - 1]).then_inc(th_in[1], 16)
            sweeps = sp.value_load(n_sweeps[0:1, 0:1], min_val=1, max_val=J)
            with sp.Fori(0, sweeps) as w:
                def load_th(blk, h):
                    sp.wait_ge(z_done, w * 2 * NB + 2 * blk + h + 1)
                    sp.dma_start(th_t[h][:], th_s[bass.ds(2 * blk + h, 1)].rearrange("o c s t -> (o c) s t")).then_inc(th_in[h], 16)

                def load_x1(blk, p):
                    sp.dma_start(x1_t[p][:], x1_s[bass.ds(blk, 1)].rearrange("o c s t -> (o c) s t")).then_inc(x1_in[p], 16)

                def store(blk, p):
                    for c in range(2):
                        sp.wait_ge(slot_free[c], w * SWEEP + blk * NG + NG + RING)
                        settle(sp)
                    src = x1_t[p][:].rearrange("c (b j) t -> c b j t", j=J)
                    for b in range(B):
                        sp.dma_start(out_v[bass.ds(blk, 1), :, b].rearrange("o c j t -> (o c) j t"), src[:, b]).then_inc(out_st[p], 16)

                def next_loads(blk, p, stored):
                    load_th(blk, 0)
                    if stored is not None:
                        sp.wait_ge(out_st[p], stored)
                        settle(sp)
                    load_x1(blk, p)
                    load_th(blk, 1)

                stores = w * (NB // 2)
                load_th(0, 0)
                load_x1(0, 0)
                load_th(0, 1)
                next_loads(1, 1, None)
                store(0, 0)
                with sp.Fori(0, (NB - 2) // 2) as k:
                    next_loads(2 * k + 2, 0, (stores + k + 1) * 16 * B)
                    store(2 * k + 1, 1)
                    next_loads(2 * k + 3, 1, (stores + k + 1) * 16 * B)
                    store(2 * k + 2, 0)
                store(NB - 1, 1)
                for p in range(2):
                    sp.wait_ge(out_st[p], (stores + NB // 2) * 16 * B)
                    settle(sp)

        def scan_tensor(pe):
            def block_steps(group, halves, start):
                def z_piece(g, u, c):
                    if g * GS + u in (0, TH) and c == 0:
                        pe.wait_ge(th_in[g * GS // TH], 16 * halves)
                    tt = g * GS + u
                    i = pe.matmul(z_b[c][g % 2][:, u * CC:(u + 1) * CC], WzT[:],
                                  th_t[tt // TH][:, c * CC:(c + 1) * CC, tt % TH], start=(u == 0), stop=False,
                                  skip_group_check=True)
                    if c == 1 and tt % TH == TH - 1:
                        i.then_inc(z_done, 1)
                for u in range(GS):
                    for c in range(2):
                        if u == 0 and start is None:
                            pe.wait_ge(y_sb[c], group * GS - GS)
                        z_piece(0, u, c)
                for g in range(NG):
                    for u in range(GS):
                        for c in range(2):
                            if g == 0 and u == 0 and start is not None:
                                pe.wait_ge(start_ok[c], start)
                                last = y_start[c][:]
                            else:
                                pe.wait_ge(y_sb[c], (group + g) * GS + u)
                                last = y[c][:, (g if u else g - 1) % RING, (u - 1) % GS, :]
                            pe.matmul(z_b[c][g % 2][:, u * CC:(u + 1) * CC], VT[:], last, start=False, stop=(u == GS - 1),
                                      skip_group_check=True).then_inc(pre_ps[c], 1)
                            if g + 1 < NG:
                                z_piece(g + 1, u, c)

            block_steps(0, 1, 1)
            sweeps = pe.value_load(n_sweeps[0:1, 0:1], min_val=1, max_val=J)
            with pe.Fori(0, sweeps) as w:
                first = w * SWEEP + NG
                block_steps(first, w * NB + 2, w + 2)
                with pe.Fori(0, NB // 2 - 1) as k:
                    for i in range(2):
                        block_steps(first + (2 * k + 1 + i) * NG, w * NB + 2 * k + 3 + i, None)
                block_steps(first + (NB - 1) * NG, w * NB + NB + 1, None)

        def scan_scalar(act):
            def block_steps(group, used):
                for g in range(NG):
                    for u in range(GS):
                        for c in range(2):
                            act.wait_ge(pre_ps[c], (group + g) * GS + u + 1)
                            if u == 0 and used is not None:
                                act.wait_ge(slot_free[c], used + g + 1)
                            act.activation(y[c][:, g % RING, u, :], z_b[c][g % 2][:, u * CC:(u + 1) * CC], ACT.Sigmoid,
                                           bias=zbias[:]).then_inc(y_sb[c], 1)

            act.wait_ge(bn_done, 1)
            block_steps(0, None)
            sweeps = act.value_load(n_sweeps[0:1, 0:1], min_val=1, max_val=J)
            with act.Fori(0, sweeps) as w:
                with act.Fori(0, NB) as k:
                    block_steps(w * SWEEP + k * NG + NG, w * SWEEP + k * NG)

        def scan_vector(dve):
            for c in range(2):
                dve.memset(y_start[c][:], 0.0).then_inc(start_ok[c], 1)
                dve.sem_inc(slot_free[c], RING)
            sweeps = dve.value_load(n_sweeps[0:1, 0:1], min_val=1, max_val=J)
            with dve.Fori(0, sweeps) as w:
                for c in range(2):
                    dve.wait_ge(y_sb[c], (w * SWEEP + NG) * GS)
                    ends = y[c][:, RING - 1, GS - 1, :].rearrange("p (b j) -> p b j", j=J)
                    dve.tensor_copy(zero_col[c][:, :, 1:J], ends[:, :, 0:J - 1]).then_inc(start_ok[c], 1)
                with dve.Fori(0, NB // 2) as k:
                    for p in range(2):
                        dve.wait_ge(x1_in[p], (w * (NB // 2) + k + 1) * 16)
                        for g in range(NG):
                            for c in range(2):
                                dve.wait_ge(y_sb[c], (w * SWEEP + (2 * k + p) * NG + NG + g + 1) * GS)
                                dst = x1_t[p][:, c * CC:(c + 1) * CC, g * GS:(g + 1) * GS]
                                dve.tensor_tensor(dst, dst, y[c][:, g % RING, :, :].rearrange("p u s -> p s u"),
                                                  ALU.add).then_inc(slot_free[c], 1)

        block = ctx.enter_context(nc.Block())

        @block.sync
        def _(sp):
            sp.dma_start(wqkv_in[:], w_qkv.rearrange("(a p) c -> p a c", p=C)).then_inc(w_in, 16)
            sp.dma_start(wout_in[:], w_out).then_inc(w_in, 16)
            sp.dma_start(W_in[:], W).then_inc(w_in, 16)
            sp.dma_start(V_in[:], V).then_inc(w_in, 16)
            sp.dma_start(cols_in[:, 0:1], gamma.rearrange("(p a) -> p a", a=1)).then_inc(w_in, 16)
            sp.dma_start(cols_in[:, 1:2], beta.rearrange("(p a) -> p a", a=1)).then_inc(w_in, 16)
            sp.dma_start(gb[:, 0, :], g.partition_broadcast(C)).then_inc(w_in, 16)
            sp.dma_start(gb[:, 1, :], b_out.partition_broadcast(C)).then_inc(w_in, 16)

            with sp.Fori(0, B) as b:
                H = NC // 2

                def load_a1(m, p):
                    sp.dma_start(xin[:, p, :], x[b, :, bass.ds((2 * m + p) * CH, CH)]).then_inc(x_in[p], 16)

                load_a1(0, 0)
                load_a1(0, 1)
                with sp.Fori(0, H - 1) as m:
                    for p in range(2):
                        sp.wait_ge(xT_ps, b * NC + 2 * m + p + 1)
                        load_a1(m + 1, p)

                def load_a2(m, p):
                    sp.dma_start(x2in[:, p, :], x[b, :, bass.ds((2 * m + p) * CH, CH)]).then_inc(x2_in[p], 16)
                    sp.dma_start(qin[:, p, :], q_image[:, bass.ds((2 * m + p) * CH, CH)]).then_inc(q_in[p], 16)

                def store_a2(m, p):
                    nb = CH // T
                    col = b * J + m
                    sp.wait_ge(x1_sb, b * NC + 2 * m + p + 1)
                    sp.dma_start(x1_s[p * nb:(p + 1) * nb, :, bass.ds(col, 1), :].rearrange("k c s t -> c k (s t)"),
                                 x1o[:, p, :].rearrange("c (k t) -> c k t", t=T)).then_inc(x1_st[p], 16)
                    sp.wait_ge(th_sb, b * NC + 2 * m + p + 1)
                    sp.dma_start(th_s[2 * p * nb:2 * (p + 1) * nb, :, bass.ds(col, 1), :].rearrange("k c s t -> c k (s t)"),
                                 tho[:, p, :].rearrange("c (k t) -> c k t", t=TH)).then_inc(th_st[p], 16)

                for p in range(2):
                    sp.wait_ge(q_kept[p], (b + 1) * H * 16)
                    settle(sp)
                load_a2(0, 0)
                load_a2(0, 1)
                with sp.Fori(0, H - 1) as m:
                    for p in range(2):
                        sp.wait_ge(o_ps, b * NC + 2 * m + p + 1)
                        load_a2(m + 1, p)
                        store_a2(m, p)
                store_a2(H - 1, 0)
                store_a2(H - 1, 1)
                for p in range(2):
                    sp.wait_ge(x1_st[p], (b + 1) * H * 16)
                    sp.wait_ge(th_st[p], (b + 1) * H * 16)
                    settle(sp)

            scan_dma(sp)

        @block.tensor
        def _(pe):
            pe.wait_ge(w_in, 8 * 16)
            pe.wait_ge(ident_ok, 1)
            srcs = [wqkv_in[:, 0, :], wqkv_in[:, 1, :], wqkv_in[:, 2, :], wout_in[:]]
            for i, s in enumerate(srcs):
                pe.transpose(bank[1][:, i * C:(i + 1) * C], s, ident[:]).then_inc(wT_ps, 1)
            for i, s in enumerate([W_in[:], V_in[:]]):
                pe.transpose(bank[2][:, i * C:(i + 1) * C], s, ident[:]).then_inc(wT_ps, 1)
            pe.wait_ge(wT_sb, 6)
            pe.matmul(bank[3][:, 0:C], VT[:], VT[:], start=True, stop=True).then_inc(wT_ps, 1)
            pe.wait_ge(cert, 1)
            pe.transpose(bank[3][0:1, C:2 * C], small[:, 0:1], ident[:]).then_inc(wT_ps, 1)
            pe.matmul(gram[:, 0:C + 1], zeros[:, 0:C], zeros[:], start=True, stop=False, skip_group_check=True)
            pe.wait_ge(setup, 1)

            with pe.Fori(0, B) as b:
                def step(n, p, has, cnt, local):
                    if has(1):
                        pe.wait_ge(x_in[1 - p], 16 * cnt(1))
                        if has(-1):
                            pe.wait_ge(ln, n)
                        for t in range(TL):
                            i = pe.transpose(xT_b[1 - p][:, t * C:(t + 1) * C], xin[:, 1 - p, t * C:(t + 1) * C], ident[:])
                        i.then_inc(xT_ps, 1)
                    if has(-2):
                        pe.wait_ge(q_nrm, n - 1)
                        if has(-3):
                            pe.wait_ge(ekT_sb, n - 2)
                        for t in range(TL):
                            i = pe.transpose(tr_b[:, t * C:(t + 1) * C], qhT[:, p, t * C:(t + 1) * C], ident[:])
                        i.then_inc(qh_ps, 1)
                    if has(0):
                        pe.wait_ge(ln, n + 1)
                        for t in range(TL):
                            i = pe.transpose(xh_b[:, t * C:(t + 1) * C], xhT[:, p, t, :], ident[:])
                        i.then_inc(xh_ps, 1)
                    if has(-1):
                        pe.wait_ge(ek_sb, n)
                        if has(-2):
                            pe.wait_ge(qh_sb, n - 1)
                        for t in range(TL):
                            i = pe.transpose(tr_b[:, t * C:(t + 1) * C], ek[:, 1 - p, t * C:(t + 1) * C], ident[:])
                        i.then_inc(ekT_ps, 1)
                    if has(0):
                        pe.wait_ge(xh_sb, n + 1)
                        pe.matmul(k_b[:], WkT[:], xh[:, p, :], start=True, stop=True).then_inc(k_ps, 1)
                        if has(-1):
                            pe.wait_ge(q_sub, n)
                        for t in range(TL):
                            i = pe.matmul(q_b[:, t * C:(t + 1) * C], xh[:, p, t * C:(t + 1) * C], WqT[:], start=True, stop=True)
                        i.then_inc(q_ps, 1)
                    if has(-1):
                        pe.wait_ge(ekT_sb, n)
                        if has(-2):
                            pe.wait_ge(g_upd, n - 1)
                        for t in range(TL):
                            i = pe.matmul(g_b[:, 0:C], ekT[:, 1 - p, t * C:(t + 1) * C], xhT[:, 1 - p, t, :],
                                          start=(t == 0), stop=(t == TL - 1))
                        i.then_inc(g_ps, 1)

                a1_steps(pe, b, step)

                pe.wait_ge(qh_sb, (b + 1) * NC)
                pe.wait_ge(q_sub, (b + 1) * NC)
                pe.wait_ge(gs_sb, b + 1)
                pe.transpose(tr_b[:, 0:C], Gs[:], ident[:]).then_inc(gT_ps, 1)
                pe.wait_ge(gT_sb, b + 1)
                pe.matmul(tr_b[:, C:2 * C], WvT[:], GT[:], start=True, stop=True).then_inc(ctx_ps, 1)
                pe.wait_ge(ctx_sb, b + 1)
                pe.matmul(g_b[:, 0:2 * C], ctxT[:], WoT[:].rearrange("p a c -> p (a c)"), start=True, stop=True).then_inc(m_ps, 1)
                pe.wait_ge(m_sb, b + 1)

                def step2(n, p, has, cnt, local):
                    if has(0):
                        pe.wait_ge(x2_in[p], 16 * cnt(0))
                        if has(-1):
                            pe.wait_ge(x2T_sb, n)
                        for t in range(TL):
                            i = pe.transpose(x2T_b[:, t * C:(t + 1) * C], x2in[:, p, t * C:(t + 1) * C], ident[:])
                        i.then_inc(x2T_ps, 1)
                        pe.wait_ge(q_in[p], 16 * cnt(0))
                        if has(-1):
                            pe.wait_ge(x1T_sb, n)
                        for t in range(TL):
                            i = pe.matmul(o_b[t // 2][:, (t % 2) * 2 * C:(t % 2 + 1) * 2 * C], qin[:, p, t * C:(t + 1) * C],
                                          MT[:].rearrange("p a c -> p (a c)"), start=True, stop=True)
                        i.then_inc(o_ps, 1)
                    if has(-1):
                        if has(-2):
                            pe.wait_ge(x1_sb, n - 1)
                        pe.wait_ge(x1T_sb, n)
                        for t in range(TL):
                            i = pe.transpose(x1_b[:, t * C:(t + 1) * C], x1T[:, 1 - p, t, :], ident[:])
                        i.then_inc(x1_ps, 1)
                        if has(-2):
                            pe.wait_ge(th_sb, n - 1)
                        pe.wait_ge(thT_sb, n)
                        for t in range(TL):
                            i = pe.transpose(th_b[:, t * C:(t + 1) * C], thT[:, 1 - p, t, 0:C], ident[:])
                        i.then_inc(th_ps, 1)
                        for t in range(TL):
                            i = pe.matmul(gram[:, 0:C + 1], thT[:, 1 - p, t, 0:C], thT[:, 1 - p, t, :], start=False, stop=False,
                                          skip_group_check=True)
                        i.then_inc(gram_ps, 1)

                a2_steps(pe, b, step2)
                pe.wait_ge(x2T_sb, (b + 1) * NC)
                pe.wait_ge(x1_sb, (b + 1) * NC)
                pe.wait_ge(th_sb, (b + 1) * NC)

            pe.wait_ge(bn_c, 1)
            pe.matmul(bank[1][:, 0:C + 1], WT[:], cov[:], start=True, stop=True).then_inc(bn_ps, 1)
            pe.wait_ge(bn_w, 1)
            pe.transpose(bank[2][:, 0:C], Wz[:], ident[:]).then_inc(bn_wps, 1)
            pe.wait_ge(bn_done, 1)
            scan_tensor(pe)

        @block.scalar
        def _(act):
            act.wait_ge(wT_ps, 6)
            for i, d in enumerate([WqT[:], WkT[:], WvT[:], WoT[:, 0, :]]):
                act.copy(d, bank[1][:, i * C:(i + 1) * C]).then_inc(wT_sb, 1)
            for i, d in enumerate([WT[:], VT[:]]):
                act.copy(d, bank[2][:, i * C:(i + 1) * C]).then_inc(wT_sb, 1)

            with act.Fori(0, B) as b:
                def step(n, p, has, cnt, local):
                    if has(-2):
                        act.wait_ge(qh_ps, n - 1)
                        if has(-4):
                            act.wait_ge(q_kept[p], 16 * cnt(-4))
                        act.copy(qh[:, p, :], tr_b[:]).then_inc(qh_sb, 1)
                    if has(-3):
                        act.wait_ge(qh_sb, n - 2)
                        act.dma_start(q_image[:, bass.ds((local - 3) * CH, CH)], qh[:, 1 - p, :]).then_inc(q_kept[1 - p], 16)
                    if has(0):
                        act.wait_ge(xh_ps, n + 1)
                        if has(-2):
                            act.wait_ge(q_ps, n - 1)
                        act.copy(xh[:, p, :], xh_b[:]).then_inc(xh_sb, 1)
                    if has(-1):
                        act.wait_ge(ekT_ps, n)
                        if has(-3):
                            act.wait_ge(g_ps, n - 2)
                        act.copy(ekT[:, 1 - p, :], tr_b[:]).then_inc(ekT_sb, 1)
                    if has(0):
                        act.wait_ge(k_max, n + 1)
                        if has(-2):
                            act.wait_ge(g_upd, n - 1)
                        act.activation(alpha[:, p:p + 1], nmax[:, 1 - p:2 - p], ACT.Exp, bias=nmax[:, p:p + 1], scale=-1.0)
                        act.activation(ek[:, p, :], k_b[:], ACT.Exp, bias=nmax[:, p:p + 1],
                                       accum_out=zc[:, p:p + 1]).then_inc(ek_sb, 1)
                    if has(1):
                        act.wait_ge(stat, n + 2)
                        if has(-1):
                            act.wait_ge(g_ps, n)
                        for t in range(TL):
                            i = act.activation(xhT[:, 1 - p, t, :], xT_b[1 - p][:, t * C:(t + 1) * C], ACT.Identity,
                                               bias=nmr[:, 1 - p, t:t + 1], scale=rstd[:, 1 - p, t:t + 1])
                        i.then_inc(ln, 1)
                    if has(0):
                        act.wait_ge(q_sub, n + 1)
                        act.activation(qs[:, p, :], qs[:, p, :], ACT.Exp).then_inc(q_exp, 1)

                a1_steps(act, b, step)

                act.wait_ge(gT_ps, b + 1)
                act.copy(GT[:], tr_b[:, 0:C]).then_inc(gT_sb, 1)

                def step2(n, p, has, cnt, local):
                    if has(0):
                        act.wait_ge(x2T_ps, n + 1)
                        if has(-2):
                            act.wait_ge(x1T_sb, n - 1)
                        act.copy(x2T[:, p, :], x2T_b[:]).then_inc(x2T_sb, 1)
                    if has(-1):
                        act.wait_ge(x1_ps, n)
                        if has(-3):
                            act.wait_ge(x1_st[1 - p], 16 * cnt(-3))
                        act.copy(x1o[:, 1 - p, :], x1_b[:]).then_inc(x1_sb, 1)
                        act.wait_ge(th_ps, n)
                        if has(-3):
                            act.wait_ge(th_st[1 - p], 16 * cnt(-3))
                        act.copy(tho[:, 1 - p, :], th_b[:]).then_inc(th_sb, 1)

                a2_steps(act, b, step2)

            scan_scalar(act)

        @block.gpsimd
        def _(pool):
            pool.memset(minus_half[:], -0.5)
            pool.memset(ident[:], 0.0).then_inc(setup_pool, 1)
            pool.wait_ge(setup_pool, 1)
            pool.affine_select(out=ident[:], in_=ident[:], compare_op=ALU.not_equal, fill=1.0, base=0,
                               pattern=[[-1, C]], channel_multiplier=1).then_inc(ident_ok, 1)
            with pool.Fori(0, B) as b:
                def step(n, p, has, cnt, local):
                    if has(1):
                        if has(-1):
                            pool.wait_ge(ln, n)
                        pool.wait_ge(x_mv, n + 2)
                        settle(pool)
                        pool.tensor_scalar(veps[:, 0, :], mv[:, 1 - p, :, 1], 1e-6, None, ALU.add).then_inc(x_var, 1)
                        pool.wait_ge(x_var, n + 2)
                        pool.tensor_tensor(rstd[:, 1 - p, :], veps[:, 0, :], minus_half[:], ALU.pow).then_inc(x_rstd, 1)
                        pool.wait_ge(x_rstd, n + 2)
                        pool.tensor_tensor(nmr[:, 1 - p, :], mv[:, 1 - p, :, 0], rstd[:, 1 - p, :], ALU.mult).then_inc(x_mr, 1)
                        pool.wait_ge(x_mr, n + 2)
                        settle(pool)
                        pool.tensor_scalar(nmr[:, 1 - p, :], nmr[:, 1 - p, :], -1.0, None, ALU.mult).then_inc(stat, 1)
                    if has(-1):
                        pool.wait_ge(q_rec, n)
                        if has(-3):
                            pool.wait_ge(qh_ps, n - 2)
                        pool.tensor_tensor(qhT[:, 1 - p, :].rearrange("q (h d) -> q h d", d=DH),
                                           qs[:, 1 - p, :].rearrange("q (h d) -> q h d", d=DH),
                                           q_inv[:, 1 - p, :].unsqueeze(2).to_broadcast([C, TL * HEADS, DH]),
                                           ALU.mult).then_inc(q_nrm, 1)

                a1_steps(pool, b, step)

                def step2(n, p, has, cnt, local):
                    if has(0):
                        pool.wait_ge(o_mv, n + 1)
                        settle(pool)
                        pool.tensor_scalar(veps[:, 1, :], omv[:, :, 1], 1e-5, None, ALU.add).then_inc(o_var, 1)
                        pool.wait_ge(o_var, n + 1)
                        pool.tensor_tensor(orstd[:], veps[:, 1, :], minus_half[:], ALU.pow).then_inc(o_rstd, 1)
                    if has(-1):
                        pool.wait_ge(s_mv, n)
                        settle(pool)
                        pool.tensor_scalar(veps[:, 2, :], smv[:, :, 1], 1e-5, None, ALU.add).then_inc(s_var, 1)
                        pool.wait_ge(s_var, n)
                        pool.tensor_tensor(srstd[:], veps[:, 2, :], minus_half[:], ALU.pow).then_inc(s_rstd, 1)
                        if has(-3):
                            pool.wait_ge(gram_ps, n - 2)
                        pool.wait_ge(s_rstd, n)
                        settle(pool)
                        for t in range(TL):
                            i = pool.tensor_scalar(thT[:, 1 - p, t, 0:C], x1T[:, 1 - p, t, :], smv[:, t, 0:1], srstd[:, t:t + 1],
                                                   ALU.subtract, ALU.mult)
                        i.then_inc(thT_sb, 1)

                a2_steps(pool, b, step2)

            pool.wait_ge(bn_var, 1)
            pool.tensor_scalar(small[:, 13:14], small[:, 9:10], 1e-5, None, ALU.add).then_inc(bn_veps, 1)
            pool.wait_ge(bn_veps, 1)
            pool.tensor_tensor(small[:, 10:11], small[:, 13:14], minus_half[:, 0:1], ALU.pow).then_inc(bn_rstd, 1)

        @block.vector
        def _(dve):
            step_n = [0]

            def chain(ins):
                step_n[0] += 1
                ins.then_inc(dve_chain, 1)
                dve.wait_ge(dve_chain, step_n[0])

            chain(dve.memset(head_mask[:], 0.0))
            for h in range(HEADS):
                dve.memset(head_mask[h * DH:(h + 1) * DH, h * DH:(h + 1) * DH], 1.0)
            dve.memset(zeros[:], 0.0)
            chain(dve.memset(thT[:, :, :, C:C + 1], 1.0))
            dve.wait_ge(w_in, 8 * 16)
            chain(dve.tensor_reduce(small[:, 3:4], gb[:, 1, :], AX, ALU.add))
            chain(dve.tensor_scalar(small[:, 4:5], small[:, 3:4], 1.0 / C, None, ALU.mult))
            chain(dve.tensor_scalar(bias_rows[:, 0, :], gb[:, 1, :], small[:, 4:5], 1.0 / HEADS, ALU.subtract, ALU.mult))
            chain(dve.tensor_tensor(bias_rows[:, 1, :], bias_rows[:, 0, :], gb[:, 0, :], ALU.mult))
            dve.wait_ge(wT_sb, 6)
            chain(dve.tensor_reduce(small[:, 1:2], WoT[:, 0, :], AX, ALU.add))
            chain(dve.tensor_scalar(small[:, 2:3], small[:, 1:2], 1.0 / C, None, ALU.mult))
            chain(dve.tensor_scalar(WoT[:, 0, :], WoT[:, 0, :], small[:, 2:3], None, ALU.subtract))
            chain(dve.tensor_tensor(WoT[:, 1, :], WoT[:, 0, :], gb[:, 0, :], ALU.mult))
            dve.wait_ge(wT_ps, 7)
            dve.tensor_reduce(small[:, 0:1], bank[3][:, 0:C], AX, ALU.add, apply_absolute_value=True).then_inc(cert, 1)
            dve.wait_ge(wT_ps, 8)
            chain(dve.tensor_reduce(cert_row[:, 0:1], bank[3][0:1, C:2 * C], AX, ALU.max))
            chain(dve.tensor_scalar(cert_row[:, 1:2], cert_row[:, 0:1], CONTRACT, None, ALU.is_le))
            dve.tensor_scalar(n_sweeps[:], cert_row[:, 1:2], float(1 - J), float(J), ALU.mult, ALU.add).then_inc(setup, 1)

            with dve.Fori(0, B) as b:
                dve.memset(nmax[:, 1:2], 3e38).then_inc(img_init, 1)
                dve.memset(Z[:], 0.0).then_inc(img_init, 1)
                dve.memset(G[:], 0.0).then_inc(img_init, 1)

                def step(n, p, has, cnt, local):
                    if has(1):
                        dve.wait_ge(xT_ps, n + 2)
                        if has(0):
                            dve.wait_ge(x_mv, n + 1)
                        for t in range(TL):
                            i = dve.bn_stats(bn6[:, 1 - p, t, :], xT_b[1 - p][:, t * C:(t + 1) * C])
                        i.then_inc(x_bn, 1)
                        if has(-1):
                            dve.wait_ge(stat, n)
                        dve.wait_ge(x_bn, n + 2)
                        settle(dve)
                        for t in range(TL):
                            i = dve.bn_aggr(mv[:, 1 - p, t, :], bn6[:, 1 - p, t, :])
                        i.then_inc(x_mv, 1)
                    if has(0):
                        dve.wait_ge(k_ps, n + 1)
                        if has(-1):
                            dve.wait_ge(k_max, n)
                        dve.tensor_reduce(ncmax[:], k_b[:], AX, ALU.max, negate=True).then_inc(kc_max, 1)
                        dve.wait_ge(kc_max, n + 1)
                        if has(-1):
                            dve.wait_ge(ek_sb, n)
                        else:
                            dve.wait_ge(img_init, 3 * b + 3)
                        dve.tensor_tensor(nmax[:, p:p + 1], nmax[:, 1 - p:2 - p], ncmax[:], ALU.min).then_inc(k_max, 1)
                        dve.wait_ge(q_ps, n + 1)
                        qv = q_b[:].rearrange("q (h d) -> q h d", d=DH)
                        if has(-1):
                            dve.wait_ge(q_sub, n)
                        dve.tensor_reduce(q_mx[:], qv, AX, ALU.max).then_inc(q_max, 1)
                        dve.wait_ge(q_max, n + 1)
                        if has(-2):
                            dve.wait_ge(q_nrm, n - 1)
                        dve.tensor_tensor(qs[:, p, :].rearrange("q (h d) -> q h d", d=DH), qv,
                                          q_mx[:].unsqueeze(2).to_broadcast([C, TL * HEADS, DH]), ALU.subtract).then_inc(q_sub, 1)
                    if has(-1):
                        dve.wait_ge(q_exp, n)
                        if has(-2):
                            dve.wait_ge(q_rec, n - 1)
                        dve.tensor_reduce(q_sum[:], qs[:, 1 - p, :].rearrange("q (h d) -> q h d", d=DH), AX, ALU.add).then_inc(q_tot, 1)
                        dve.wait_ge(q_tot, n)
                        dve.reciprocal(q_inv[:, 1 - p, :], q_sum[:]).then_inc(q_rec, 1)
                        dve.wait_ge(ek_sb, n)
                        if has(-2):
                            dve.wait_ge(z_upd, n - 1)
                        dve.scalar_tensor_tensor(Z[:], Z[:], alpha[:, 1 - p:2 - p], zc[:, 1 - p:2 - p],
                                                 ALU.mult, ALU.add).then_inc(z_upd, 1)
                        dve.wait_ge(g_ps, n)
                        if has(-2):
                            dve.wait_ge(g_upd, n - 1)
                        dve.scalar_tensor_tensor(G[:], G[:], alpha[:, 1 - p:2 - p], g_b[:, 0:C],
                                                 ALU.mult, ALU.add).then_inc(g_upd, 1)

                a1_steps(dve, b, step)

                dve.wait_ge(z_upd, (b + 1) * NC)
                dve.reciprocal(small[:, 5:6], Z[:]).then_inc(img_rz, 1)
                dve.wait_ge(img_rz, b + 1)
                dve.wait_ge(g_upd, (b + 1) * NC)
                dve.tensor_scalar(Gs[:], G[:], small[:, 5:6], DH ** -0.5 / N, ALU.mult, ALU.mult).then_inc(gs_sb, 1)
                dve.wait_ge(ctx_ps, b + 1)
                dve.tensor_tensor(ctxT[:], tr_b[:, C:2 * C], head_mask[:], ALU.mult).then_inc(ctx_sb, 1)
                dve.wait_ge(m_ps, b + 1)
                dve.tensor_tensor(MT[:].rearrange("p a c -> p (a c)"), g_b[:, 0:2 * C],
                                  bias_rows[:].rearrange("p a c -> p (a c)"), ALU.add).then_inc(m_sb, 1)

                def step2(n, p, has, cnt, local):
                    if has(0):
                        dve.wait_ge(o_ps, n + 1)
                        if has(-1):
                            dve.wait_ge(o_mv, n)
                        for t in range(TL):
                            at = (t % 2) * 2 * C
                            i = dve.bn_stats(o6[:, t, :], o_b[t // 2][:, at:at + C])
                        i.then_inc(o_bn, 1)
                        dve.wait_ge(o_bn, n + 1)
                        settle(dve)
                        for t in range(TL):
                            i = dve.bn_aggr(omv[:, t, :], o6[:, t, :])
                        i.then_inc(o_mv, 1)
                    if has(-1):
                        dve.wait_ge(x1T_sb, n)
                        if has(-2):
                            dve.wait_ge(s_mv, n - 1)
                        for t in range(TL):
                            i = dve.bn_stats(s6[:, t, :], x1T[:, 1 - p, t, :])
                        i.then_inc(s_bn, 1)
                        if has(-2):
                            dve.wait_ge(thT_sb, n - 1)
                        dve.wait_ge(s_bn, n)
                        settle(dve)
                        for t in range(TL):
                            i = dve.bn_aggr(smv[:, t, :], s6[:, t, :])
                        i.then_inc(s_mv, 1)
                    if has(0):
                        dve.wait_ge(x2T_sb, n + 1)
                        if has(-2):
                            dve.wait_ge(x1_ps, n - 1)
                            dve.wait_ge(thT_sb, n - 1)
                        dve.wait_ge(o_rstd, n + 1)
                        for t in range(TL):
                            at = (t % 2) * 2 * C + C
                            i = dve.scalar_tensor_tensor(x1T[:, p, t, :], o_b[t // 2][:, at:at + C], orstd[:, t:t + 1],
                                                         x2T[:, p, t * C:(t + 1) * C], ALU.mult, ALU.add)
                        i.then_inc(x1T_sb, 1)

                a2_steps(dve, b, step2)

            dve.wait_ge(gram_ps, B * NC)
            dve.tensor_scalar(cov[:], gram[:, 0:C + 1], 1.0 / TOK, None, ALU.mult).then_inc(bn_c, 1)
            dve.wait_ge(bn_ps, 1)
            chain(dve.tensor_tensor(tmp[:], bank[1][:, 0:C], W_in[:], ALU.mult))
            chain(dve.tensor_reduce(small[:, 6:7], tmp[:], AX, ALU.add))
            chain(dve.tensor_copy(small[:, 7:8], bank[1][:, C:C + 1]))
            chain(dve.tensor_tensor(small[:, 8:9], small[:, 7:8], small[:, 7:8], ALU.mult))
            dve.tensor_tensor(small[:, 9:10], small[:, 6:7], small[:, 8:9], ALU.subtract).then_inc(bn_var, 1)
            dve.wait_ge(bn_rstd, 1)
            chain(dve.tensor_tensor(small[:, 11:12], small[:, 10:11], cols_in[:, 0:1], ALU.mult))
            dve.tensor_scalar(Wz[:], W_in[:], small[:, 11:12], None, ALU.mult).then_inc(bn_w, 1)
            chain(dve.tensor_tensor(small[:, 12:13], small[:, 7:8], small[:, 11:12], ALU.mult))
            chain(dve.tensor_tensor(zbias[:], cols_in[:, 1:2], small[:, 12:13], ALU.subtract))
            dve.wait_ge(bn_wps, 1)
            dve.tensor_copy(WzT[:], bank[2][:, 0:C]).then_inc(bn_done, 1)
            scan_vector(dve)

_INS = ["x", "L0_conv_w_qkv", "L0_conv_w_out", "L0_conv_g", "L0_conv_b_out", "L0_ffn_W", "L0_ffn_V", "L0_ffn_gamma", "L0_ffn_beta"]


def program(nc, shapes):
    t = {n: nc.dram_tensor(f"in_{n}", s, F32, kind="ExternalInput").ap() for n, s in shapes.items()}
    out = nc.dram_tensor("out", shapes["x"], F32, kind="ExternalOutput").ap()
    build(nc, t["x"].rearrange("b c h w -> b c (h w)"), t["L0_conv_w_qkv"], t["L0_conv_w_out"], t["L0_conv_b_out"],
          t["L0_conv_g"], t["L0_ffn_W"], t["L0_ffn_V"], t["L0_ffn_gamma"], t["L0_ffn_beta"],
          out.rearrange("b c h w -> b c (h w)"))


def kernel(**inputs):
    import concourse.bacc as bacc
    from concourse.bass_utils import run_bass_kernel_spmd

    nc = bacc.Bacc("TRN2", target_bir_lowering=False, num_devices=1)
    arrays = {n: np.ascontiguousarray(inputs[n]) for n in _INS}
    program(nc, {n: arrays[n].shape for n in _INS})
    r = run_bass_kernel_spmd(nc, [{f"in_{n}": arrays[n] for n in _INS}], core_ids=[0])
    return r.results[0]["out"]
```

```python
import numpy as np
import concourse.bass as bass
from concourse import mybir
from contextlib import ExitStack

F32 = mybir.dt.float32
I32 = mybir.dt.int32
ALU = mybir.AluOpType
ACT = mybir.ActivationFunctionType
AX = mybir.AxisListType.X

C = 128
HEADS = 4
DH = C // HEADS
CH = 512
TL = CH // 128
SEG = 1024
T = 64
TH = T // 2
GS = 4
NG = T // GS
RING = 2
CONTRACT = 1.01
HEAD = 8


def build(nc, x, w_qkv, w_out, b_out, g, W, V, gamma, beta, out):
    B, _, N = x.shape
    NC = N // CH
    J = N // SEG
    NB = SEG // T
    COLS = B * J
    CC = COLS // 2
    TOK = B * N
    assert NC % 4 == 0 and NC > HEAD and B >= 2 and NB % 2 == 0 and CC * GS <= 512 and RING * GS <= T

    x1_s = nc.dram_tensor("x1_scratch", (NB, C, COLS, T), F32).ap()
    th_s = nc.dram_tensor("th_scratch", (2 * NB, C, COLS, TH), F32).ap()

    with ExitStack() as ctx:
        def sem(name):
            return ctx.enter_context(nc.semaphore(name))

        def sb(name, shape, dt=F32, stack=ctx):
            return stack.enter_context(nc.sbuf_tensor(name, shape, dt))

        bank = [ctx.enter_context(nc.psum_tensor(f"bank{i}", [C, 512], F32)) for i in range(8)]

        ident = sb("ident", [C, C])
        VT = sb("VT", [C, C])
        WzT = sb("WzT", [C, C])
        zbias = sb("zbias", [C, 1])
        y = [sb(f"y{c}", [C, RING, GS, CC]) for c in range(2)]
        y_start = [sb(f"y_start{c}", [C, CC]) for c in range(2)]
        n_sweeps = sb("n_sweeps", [1, 1], I32)

        w_in, ident_ok = sem("w_in"), sem("ident_ok")
        wT_ps, cert = sem("wT_ps"), sem("cert")
        wT_sb, setup, setup_pool, dve_chain = (sem(s) for s in ("wT_sb", "setup", "setup_pool", "dve_chain"))
        x_in = [sem(f"x_in{i}") for i in range(4)]
        xT_ps, x_bn, x_mv, x_var, x_rstd, x_mr, stat, ln = (
            sem(s) for s in ("xT_ps", "x_bn", "x_mv", "x_var", "x_rstd", "x_mr", "stat", "ln"))
        xh_ps, xh_sb, k_ps, kc_max, k_max, ek_sb, ekT_ps, ekT_sb, g_ps, z_upd, g_upd = (
            sem(s) for s in ("xh_ps", "xh_sb", "k_ps", "kc_max", "k_max", "ek_sb", "ekT_ps", "ekT_sb", "g_ps", "z_upd", "g_upd"))
        q_ps, q_max, q_sub, q_exp, q_tot, q_rec, q_nrm, qh_ps, qh_sb = (
            sem(s) for s in ("q_ps", "q_max", "q_sub", "q_exp", "q_tot", "q_rec", "q_nrm", "qh_ps", "qh_sb"))
        q_kept = [sem(f"q_kept{i}") for i in range(2)]
        img_init, img_rz, gs_sb, gT_ps, gT_sb, ctx_ps, ctx_sb, m_ps, m_sb = (
            sem(s) for s in ("img_init", "img_rz", "gs_sb", "gT_ps", "gT_sb", "ctx_ps", "ctx_sb", "m_ps", "m_sb"))
        x2_in = [sem(f"x2_in{i}") for i in range(4)]
        q_in = [sem(f"q_in{i}") for i in range(4)]
        o_ps, o_sq, o_var, o_rstd, o_nrm, on_ps, x1_sb, x1T_ps, s_bn, s_mv, s_var, s_rstd, thT_sb, gram_ps, th_ps, th_sb = (
            sem(s) for s in ("o_ps", "o_sq", "o_var", "o_rstd", "o_nrm", "on_ps", "x1_sb", "x1T_ps", "s_bn", "s_mv", "s_var",
                             "s_rstd", "thT_sb", "gram_ps", "th_ps", "th_sb"))
        x1_st = [sem(f"x1_st{i}") for i in range(4)]
        th_st = [sem(f"th_st{i}") for i in range(2)]
        bn_c, bn_ps, bn_var, bn_veps, bn_rstd, bn_w, bn_wps, bn_done = (
            sem(s) for s in ("bn_c", "bn_ps", "bn_var", "bn_veps", "bn_rstd", "bn_w", "bn_wps", "bn_done"))
        settled = {e.engine: sem(f"settled_{n}") for n, e in (("sp", nc.sync), ("pool", nc.gpsimd), ("dve", nc.vector))}
        th_in = [sem(f"th_in{h}") for h in range(2)]
        x1_in = [sem(f"x1_in{p}") for p in range(2)]
        out_st = [sem(f"out_st{p}") for p in range(2)]
        start_ok = [sem(f"start_ok{c}") for c in range(2)]
        z_done = sem("z_done")
        pre_ps = [sem(f"pre_ps{c}") for c in range(2)]
        y_sb = [sem(f"y_sb{c}") for c in range(2)]
        slot_free = [sem(f"slot_free{c}") for c in range(2)]

        a = ExitStack()

        def sa(name, shape, dt=F32):
            return sb(name, shape, dt, a)

        wqkv_in = sa("wqkv_in", [C, 3, C])
        wout_in = sa("wout_in", [C, C])
        W_in = sa("W_in", [C, C])
        V_in = sa("V_in", [C, C])
        cols_in = sa("cols_in", [C, 3])
        b_rows = sa("b_rows", [C, C])
        WqT, WkT, WvT = sa("WqT", [C, C]), sa("WkT", [C, C]), sa("WvT", [C, C])
        WoT = sa("WoT", [C, C])
        bias_rows = sa("bias_rows", [C, C])
        WT = sa("WT", [C, C])
        head_mask = sa("head_mask", [C, C])
        tmp = sa("tmp", [C, C])
        small = sa("small", [C, 16])
        cert_row = sa("cert_row", [1, 4])
        minus_half = sa("minus_half", [C, TL])
        veps = sa("veps", [C, 3, TL])
        zeros = sa("zeros", [C, C + 1])

        xin = sa("xin", [C, 4, CH])
        bn6 = sa("bn6", [C, TL, 6])
        mv = sa("mv", [C, 2, TL, 2])
        rstd = sa("rstd", [C, 2, TL])
        nmr = sa("nmr", [C, 2, TL])
        mr = sa("mr", [C, TL])
        xhT = sa("xhT", [C, 4, TL, C])
        xh = sa("xh", [C, 2, CH])
        nmax = sa("nmax", [C, 2])
        ncmax = sa("ncmax", [C, 1])
        alpha = sa("alpha", [C, 4])
        zc = sa("zc", [C, 4])
        Z = sa("Z", [C, 1])
        G = sa("G", [C, C])
        Gs = sa("Gs", [C, C])
        GT = sa("GT", [C, C])
        ctxT = sa("ctxT", [C, C])
        MT = sa("MT", [C, C])
        ek = sa("ek", [C, 2, CH])
        ekT = sa("ekT", [C, 2, CH])
        q_mx = sa("q_mx", [C, TL * HEADS])
        qs = sa("qs", [C, 4, CH])
        q_sum = sa("q_sum", [C, TL * HEADS])
        q_inv = sa("q_inv", [C, 2, TL * HEADS])
        qhT = sa("qhT", [C, 2, CH])
        qh = sa("qh", [C, 2, CH])
        q_image = sa("q_image", [C, N])

        x2in = sa("x2in", [C, 4, CH])
        qin = sa("qin", [C, 4, CH])
        sq = sa("sq", [C, 2, CH])
        ssq = sa("ssq", [C, 2, TL])
        orstd = sa("orstd", [C, 2, TL])
        onT = sa("onT", [C, 2, CH])
        s6 = sa("s6", [C, TL, 6])
        smv = sa("smv", [C, 2, TL, 2])
        srstd = sa("srstd", [C, 2, TL])
        thT = sa("thT", [C, 2, TL, C + 1])
        x1o = sa("x1o", [C, 4, CH])
        tho = sa("tho", [C, 2, CH])
        cov = sa("cov", [C, C + 1])
        Wz = sa("Wz", [C, C])

        gram = bank[0]
        xT_b = [bank[1], bank[2]]
        xh_b, k_b, q_b, tr_b, g_b = bank[3], bank[4], bank[5], bank[6], bank[7]
        o_b, on_b, x1T_b, th_b = [bank[1], bank[2]], bank[3], [bank[4], bank[5]], bank[6]

        def settle(eng):
            eng.sem_inc(settled[eng.engine], 1)

        class Step:
            def __init__(self, b, s, k=None):
                self.b, self.s, self.k = b, s, k

            def has(self, lag):
                if self.k is None:
                    return 0 <= self.s - lag < NC
                assert self.s >= lag
                return True

            def local(self, lag):
                return self.s - lag if self.k is None else self.k * 4 + (self.s - lag)

            def upto(self, lag):
                return self.b * NC + self.local(lag) + 1

            def slot(self, lag, ring):
                return (self.s - lag) % ring

            def in_slot(self, lag, ring):
                c = (self.s - lag) // ring + 1
                return self.b * (NC // ring) + (c if self.k is None else c + self.k * (4 // ring))

        def image(eng, b, emit, depth):
            for s in range(HEAD):
                emit(Step(b, s))
            with eng.Fori(0, (NC - HEAD) // 4) as k:
                for s in range(HEAD, HEAD + 4):
                    emit(Step(b, s, k))
            for s in range(NC, NC + depth):
                emit(Step(b, s))

        A1_DEPTH, A2_DEPTH = 5, 5

        a.close()
        th_t = [sb(f"th_t{h}", [C, COLS, TH]) for h in range(2)]
        x1_t = [sb(f"x1_t{p}", [C, COLS, T]) for p in range(2)]
        z_b = [[bank[1], bank[2]], [bank[3], bank[4]]]
        out_v = out.rearrange("b c (j k t) -> k c b j t", k=NB, t=T)
        SWEEP = NB * NG
        zero_col = [yb[:].rearrange("p (b j) -> p b j", j=J) for yb in y_start]

        def scan_dma(sp):
            sp.wait_ge(bn_done, 1)
            sp.dma_start(th_t[0][:], th_s[2 * NB - 2]).then_inc(th_in[0], 16)
            sp.dma_start(th_t[1][:], th_s[2 * NB - 1]).then_inc(th_in[1], 16)
            sweeps = sp.value_load(n_sweeps[0:1, 0:1], min_val=1, max_val=J)
            with sp.Fori(0, sweeps) as w:
                def load_th(blk, h):
                    sp.wait_ge(z_done, w * 2 * NB + 2 * blk + h + 1)
                    sp.dma_start(th_t[h][:], th_s[bass.ds(2 * blk + h, 1)].rearrange("o c s t -> (o c) s t")).then_inc(th_in[h], 16)

                def load_x1(blk, p):
                    sp.dma_start(x1_t[p][:], x1_s[bass.ds(blk, 1)].rearrange("o c s t -> (o c) s t")).then_inc(x1_in[p], 16)

                def store(blk, p):
                    for c in range(2):
                        sp.wait_ge(slot_free[c], w * SWEEP + blk * NG + NG + RING)
                        settle(sp)
                    src = x1_t[p][:].rearrange("c (b j) t -> c b j t", j=J)
                    for b in range(B):
                        sp.dma_start(out_v[bass.ds(blk, 1), :, b].rearrange("o c j t -> (o c) j t"), src[:, b]).then_inc(out_st[p], 16)

                def next_loads(blk, p, stored):
                    load_th(blk, 0)
                    if stored is not None:
                        sp.wait_ge(out_st[p], stored)
                        settle(sp)
                    load_x1(blk, p)
                    load_th(blk, 1)

                stores = w * (NB // 2)
                load_th(0, 0)
                load_x1(0, 0)
                load_th(0, 1)
                next_loads(1, 1, None)
                store(0, 0)
                with sp.Fori(0, (NB - 2) // 2) as k:
                    next_loads(2 * k + 2, 0, (stores + k + 1) * 16 * B)
                    store(2 * k + 1, 1)
                    next_loads(2 * k + 3, 1, (stores + k + 1) * 16 * B)
                    store(2 * k + 2, 0)
                store(NB - 1, 1)
                for p in range(2):
                    sp.wait_ge(out_st[p], (stores + NB // 2) * 16 * B)
                    settle(sp)

        def scan_tensor(pe):
            def block_steps(group, halves, start):
                def z_piece(g, u, c):
                    if g * GS + u in (0, TH) and c == 0:
                        pe.wait_ge(th_in[g * GS // TH], 16 * halves)
                    tt = g * GS + u
                    i = pe.matmul(z_b[c][g % 2][:, u * CC:(u + 1) * CC], WzT[:],
                                  th_t[tt // TH][:, c * CC:(c + 1) * CC, tt % TH], start=(u == 0), stop=False,
                                  skip_group_check=True)
                    if c == 1 and tt % TH == TH - 1:
                        i.then_inc(z_done, 1)
                for u in range(GS):
                    for c in range(2):
                        if u == 0 and start is None:
                            pe.wait_ge(y_sb[c], group * GS - GS)
                        z_piece(0, u, c)
                for g in range(NG):
                    for u in range(GS):
                        for c in range(2):
                            if g == 0 and u == 0 and start is not None:
                                pe.wait_ge(start_ok[c], start)
                                last = y_start[c][:]
                            else:
                                pe.wait_ge(y_sb[c], (group + g) * GS + u)
                                last = y[c][:, (g if u else g - 1) % RING, (u - 1) % GS, :]
                            pe.matmul(z_b[c][g % 2][:, u * CC:(u + 1) * CC], VT[:], last, start=False, stop=(u == GS - 1),
                                      skip_group_check=True).then_inc(pre_ps[c], 1)
                            if g + 1 < NG:
                                z_piece(g + 1, u, c)

            block_steps(0, 1, 1)
            sweeps = pe.value_load(n_sweeps[0:1, 0:1], min_val=1, max_val=J)
            with pe.Fori(0, sweeps) as w:
                first = w * SWEEP + NG
                block_steps(first, w * NB + 2, w + 2)
                with pe.Fori(0, NB // 2 - 1) as k:
                    for i in range(2):
                        block_steps(first + (2 * k + 1 + i) * NG, w * NB + 2 * k + 3 + i, None)
                block_steps(first + (NB - 1) * NG, w * NB + NB + 1, None)

        def scan_scalar(act):
            def block_steps(group, used):
                for g in range(NG):
                    for u in range(GS):
                        for c in range(2):
                            act.wait_ge(pre_ps[c], (group + g) * GS + u + 1)
                            if u == 0 and used is not None:
                                act.wait_ge(slot_free[c], used + g + 1)
                            act.activation(y[c][:, g % RING, u, :], z_b[c][g % 2][:, u * CC:(u + 1) * CC], ACT.Sigmoid,
                                           bias=zbias[:]).then_inc(y_sb[c], 1)

            act.wait_ge(bn_done, 1)
            block_steps(0, None)
            sweeps = act.value_load(n_sweeps[0:1, 0:1], min_val=1, max_val=J)
            with act.Fori(0, sweeps) as w:
                with act.Fori(0, NB) as k:
                    block_steps(w * SWEEP + k * NG + NG, w * SWEEP + k * NG)

        def scan_vector(dve):
            for c in range(2):
                dve.memset(y_start[c][:], 0.0).then_inc(start_ok[c], 1)
                dve.sem_inc(slot_free[c], RING)
            sweeps = dve.value_load(n_sweeps[0:1, 0:1], min_val=1, max_val=J)
            with dve.Fori(0, sweeps) as w:
                for c in range(2):
                    dve.wait_ge(y_sb[c], (w * SWEEP + NG) * GS)
                    ends = y[c][:, RING - 1, GS - 1, :].rearrange("p (b j) -> p b j", j=J)
                    dve.tensor_copy(zero_col[c][:, :, 1:J], ends[:, :, 0:J - 1]).then_inc(start_ok[c], 1)
                with dve.Fori(0, NB // 2) as k:
                    for p in range(2):
                        dve.wait_ge(x1_in[p], (w * (NB // 2) + k + 1) * 16)
                        for g in range(NG):
                            for c in range(2):
                                dve.wait_ge(y_sb[c], (w * SWEEP + (2 * k + p) * NG + NG + g + 1) * GS)
                                dst = x1_t[p][:, c * CC:(c + 1) * CC, g * GS:(g + 1) * GS]
                                dve.tensor_tensor(dst, dst, y[c][:, g % RING, :, :].rearrange("p u s -> p s u"),
                                                  ALU.add).then_inc(slot_free[c], 1)

        block = ctx.enter_context(nc.Block())

        @block.sync
        def _(sp):
            sp.dma_start(wqkv_in[:], w_qkv.rearrange("(a p) c -> p a c", p=C)).then_inc(w_in, 16)
            sp.dma_start(wout_in[:], w_out).then_inc(w_in, 16)
            sp.dma_start(W_in[:], W).then_inc(w_in, 16)
            sp.dma_start(V_in[:], V).then_inc(w_in, 16)
            sp.dma_start(cols_in[:, 0:1], gamma.rearrange("(p a) -> p a", a=1)).then_inc(w_in, 16)
            sp.dma_start(cols_in[:, 1:2], beta.rearrange("(p a) -> p a", a=1)).then_inc(w_in, 16)
            sp.dma_start(cols_in[:, 2:3], g.rearrange("(p a) -> p a", a=1)).then_inc(w_in, 16)
            sp.dma_start(b_rows[:], b_out.partition_broadcast(C)).then_inc(w_in, 16)

            H = NC // 4

            def load_a1(b, m, u):
                sp.dma_start(xin[:, u, :], x[b, :, bass.ds((4 * m + u) * CH, CH)]).then_inc(x_in[u], 16)

            def load_x2(b, m, u):
                sp.dma_start(x2in[:, u, :], x[b, :, bass.ds((4 * m + u) * CH, CH)]).then_inc(x2_in[u], 16)

            def load_q(m, u):
                sp.dma_start(qin[:, u, :], q_image[:, bass.ds((4 * m + u) * CH, CH)]).then_inc(q_in[u], 16)

            def store_x1(b, m, u):
                nb = CH // T
                sp.wait_ge(x1_sb, b * NC + 4 * m + u + 1)
                sp.dma_start(x1_s[u % 2 * nb:(u % 2 + 1) * nb, :, bass.ds(b * J + 2 * m + u // 2, 1), :].rearrange("k c s t -> c k (s t)"),
                             x1o[:, u, :].rearrange("c (k t) -> c k t", t=T)).then_inc(x1_st[u], 16)

            def store_th(b, m, u):
                nb = CH // TH
                sp.wait_ge(th_sb, b * NC + 4 * m + u + 1)
                sp.dma_start(th_s[u % 2 * nb:(u % 2 + 1) * nb, :, bass.ds(b * J + 2 * m + u // 2, 1), :].rearrange("k c s t -> c k (s t)"),
                             tho[:, u % 2, :].rearrange("c (k t) -> c k t", t=TH)).then_inc(th_st[u % 2], 16)

            def one_image(b, first, last):
                with sp.Fori(0, H - 1) as m:
                    for u in range(4):
                        sp.wait_ge(xT_ps, b * NC + 4 * m + u + 1)
                        load_a1(b, m + 1, u)
                for u in range(4):
                    load_x2(b, 0, u)
                if not first:
                    for u in range(4):
                        sp.wait_ge(x1_st[u], b * H * 16)
                        settle(sp)
                    for u in range(2):
                        sp.wait_ge(th_st[u], b * H * 32)
                        settle(sp)
                for u in range(2):
                    sp.wait_ge(q_kept[u], (b + 1) * H * 32)
                    settle(sp)
                for u in range(4):
                    load_q(0, u)
                if not last:
                    for u in range(4):
                        load_a1(b + 1, 0, u)

                def turn(m, u, th):
                    sp.wait_ge(o_ps, b * NC + 4 * m + u + 1)
                    load_q(m + 1, u)
                    if th:
                        store_th(b, m - 1, u)
                    store_x1(b, m, u)
                    load_x2(b, m + 1, u)

                for u in range(4):
                    turn(0, u, False)
                with sp.Fori(1, H - 1) as m:
                    for u in range(4):
                        turn(m, u, True)
                for u in range(4):
                    store_th(b, H - 2, u)
                    store_x1(b, H - 1, u)
                for u in range(4):
                    store_th(b, H - 1, u)

            for u in range(4):
                load_a1(0, 0, u)
            one_image(0, True, B == 1)
            if B > 2:
                with sp.Fori(1, B - 1) as b:
                    one_image(b, False, False)
            one_image(B - 1, False, True)
            for u in range(4):
                sp.wait_ge(x1_st[u], B * H * 16)
            for u in range(2):
                sp.wait_ge(th_st[u], B * H * 32)
            scan_dma(sp)

        @block.tensor
        def _(pe):
            pe.wait_ge(w_in, 8 * 16)
            pe.wait_ge(ident_ok, 1)
            srcs = [wqkv_in[:, 0, :], wqkv_in[:, 1, :], wqkv_in[:, 2, :], wout_in[:]]
            for i, s in enumerate(srcs):
                pe.transpose(bank[1][:, i * C:(i + 1) * C], s, ident[:]).then_inc(wT_ps, 1)
            for i, s in enumerate([W_in[:], V_in[:]]):
                pe.transpose(bank[2][:, i * C:(i + 1) * C], s, ident[:]).then_inc(wT_ps, 1)
            pe.wait_ge(wT_sb, 6)
            pe.matmul(bank[3][:, 0:C], VT[:], VT[:], start=True, stop=True).then_inc(wT_ps, 1)
            pe.wait_ge(cert, 1)
            pe.transpose(bank[3][0:1, C:2 * C], small[:, 0:1], ident[:]).then_inc(wT_ps, 1)
            pe.matmul(gram[:, 0:C + 1], zeros[:, 0:C], zeros[:], start=True, stop=False, skip_group_check=True)
            pe.wait_ge(setup, 1)

            with pe.Fori(0, B) as b:
                def step(S):
                    if S.has(0):
                        pe.wait_ge(x_in[S.slot(0, 4)], 16 * S.in_slot(0, 4))
                        if S.has(2):
                            pe.wait_ge(ln, S.upto(2))
                        for t in range(TL):
                            i = pe.transpose(xT_b[S.slot(0, 2)][:, t * C:(t + 1) * C], xin[:, S.slot(0, 4), t * C:(t + 1) * C], ident[:])
                        i.then_inc(xT_ps, 1)
                    if S.has(2):
                        pe.wait_ge(xh_sb, S.upto(2))
                        if S.has(3):
                            pe.wait_ge(ek_sb, S.upto(3))
                        pe.matmul(k_b[:], WkT[:], xh[:, S.slot(2, 2), :], start=True, stop=True).then_inc(k_ps, 1)
                        if S.has(3):
                            pe.wait_ge(q_sub, S.upto(3))
                        for t in range(TL):
                            i = pe.matmul(q_b[:, t * C:(t + 1) * C], xh[:, S.slot(2, 2), t * C:(t + 1) * C], WqT[:], start=True, stop=True)
                        i.then_inc(q_ps, 1)
                    if S.has(3):
                        pe.wait_ge(ek_sb, S.upto(3))
                        if S.has(5):
                            pe.wait_ge(qh_sb, S.upto(5))
                        for t in range(TL):
                            i = pe.transpose(tr_b[:, t * C:(t + 1) * C], ek[:, S.slot(3, 2), t * C:(t + 1) * C], ident[:])
                        i.then_inc(ekT_ps, 1)
                    if S.has(1):
                        pe.wait_ge(ln, S.upto(1))
                        for t in range(TL):
                            i = pe.transpose(xh_b[:, t * C:(t + 1) * C], xhT[:, S.slot(1, 4), t, :], ident[:])
                        i.then_inc(xh_ps, 1)
                    if S.has(3):
                        pe.wait_ge(ekT_sb, S.upto(3))
                        if S.has(4):
                            pe.wait_ge(g_upd, S.upto(4))
                        for t in range(TL):
                            i = pe.matmul(g_b[:, 0:C], ekT[:, S.slot(3, 2), t * C:(t + 1) * C], xhT[:, S.slot(3, 4), t, :],
                                          start=(t == 0), stop=(t == TL - 1))
                        i.then_inc(g_ps, 1)
                    if S.has(4):
                        if not S.has(3):
                            pe.wait_ge(qh_sb, S.upto(5))
                        pe.wait_ge(q_nrm, S.upto(4))
                        for t in range(TL):
                            i = pe.transpose(tr_b[:, t * C:(t + 1) * C], qhT[:, S.slot(4, 2), t * C:(t + 1) * C], ident[:])
                        i.then_inc(qh_ps, 1)

                image(pe, b, step, A1_DEPTH)

                pe.wait_ge(qh_sb, (b + 1) * NC)
                pe.wait_ge(q_sub, (b + 1) * NC)
                pe.wait_ge(gs_sb, b + 1)
                pe.transpose(tr_b[:, 0:C], Gs[:], ident[:]).then_inc(gT_ps, 1)
                pe.wait_ge(gT_sb, b + 1)
                pe.matmul(tr_b[:, C:2 * C], WvT[:], GT[:], start=True, stop=True).then_inc(ctx_ps, 1)
                pe.wait_ge(ctx_sb, b + 1)
                pe.matmul(g_b[:, 0:C], ctxT[:], WoT[:], start=True, stop=True).then_inc(m_ps, 1)
                pe.wait_ge(m_sb, b + 1)

                def step2(S):
                    if S.has(0):
                        pe.wait_ge(q_in[S.slot(0, 4)], 16 * S.in_slot(0, 4))
                        if S.has(2):
                            pe.wait_ge(o_nrm, S.upto(2))
                        for t in range(TL):
                            i = pe.matmul(o_b[S.slot(0, 2)][:, t * C:(t + 1) * C], qin[:, S.slot(0, 4), t * C:(t + 1) * C], MT[:],
                                          start=True, stop=True)
                        i.then_inc(o_ps, 1)
                    if S.has(1):
                        pe.wait_ge(o_nrm, S.upto(1))
                        if S.has(2):
                            pe.wait_ge(x1_sb, S.upto(2))
                        for t in range(TL):
                            i = pe.transpose(on_b[:, t * C:(t + 1) * C], onT[:, S.slot(1, 2), t * C:(t + 1) * C], ident[:])
                        i.then_inc(on_ps, 1)
                    if S.has(2):
                        pe.wait_ge(x1_sb, S.upto(2))
                        if S.has(4):
                            pe.wait_ge(thT_sb, S.upto(4))
                        for t in range(TL):
                            i = pe.transpose(x1T_b[S.slot(2, 2)][:, t * C:(t + 1) * C], x1o[:, S.slot(2, 4), t * C:(t + 1) * C], ident[:])
                        i.then_inc(x1T_ps, 1)
                    if S.has(4):
                        pe.wait_ge(thT_sb, S.upto(4))
                        for t in range(TL):
                            i = pe.matmul(gram[:, 0:C + 1], thT[:, S.slot(4, 2), t, 0:C], thT[:, S.slot(4, 2), t, :], start=False, stop=False,
                                          skip_group_check=True)
                        i.then_inc(gram_ps, 1)
                        if S.has(5):
                            pe.wait_ge(th_sb, S.upto(5))
                        for t in range(TL):
                            i = pe.transpose(th_b[:, t * C:(t + 1) * C], thT[:, S.slot(4, 2), t, 0:C], ident[:])
                        i.then_inc(th_ps, 1)

                image(pe, b, step2, A2_DEPTH)
                pe.wait_ge(th_sb, (b + 1) * NC)

            pe.wait_ge(bn_c, 1)
            pe.matmul(bank[1][:, 0:C + 1], WT[:], cov[:], start=True, stop=True).then_inc(bn_ps, 1)
            pe.wait_ge(bn_w, 1)
            pe.transpose(bank[2][:, 0:C], Wz[:], ident[:]).then_inc(bn_wps, 1)
            pe.wait_ge(bn_done, 1)
            scan_tensor(pe)

        @block.scalar
        def _(act):
            act.wait_ge(wT_ps, 6)
            for i, d in enumerate([WqT[:], WkT[:], WvT[:], WoT[:]]):
                act.copy(d, bank[1][:, i * C:(i + 1) * C]).then_inc(wT_sb, 1)
            for i, d in enumerate([WT[:], VT[:]]):
                act.copy(d, bank[2][:, i * C:(i + 1) * C]).then_inc(wT_sb, 1)

            with act.Fori(0, B) as b:
                def step(S):
                    if S.has(5):
                        act.wait_ge(qh_sb, S.upto(5))
                        act.dma_start(q_image[:, bass.ds(S.local(5) * CH, CH)], qh[:, S.slot(5, 2), :]).then_inc(q_kept[S.slot(5, 2)], 16)
                    if S.has(3):
                        act.wait_ge(ekT_ps, S.upto(3))
                        if S.has(5):
                            act.wait_ge(g_ps, S.upto(5))
                        act.copy(ekT[:, S.slot(3, 2), :], tr_b[:]).then_inc(ekT_sb, 1)
                    if S.has(2):
                        act.wait_ge(k_max, S.upto(2))
                        if S.has(6):
                            act.wait_ge(g_upd, S.upto(6))
                        a4, p = S.slot(2, 4), S.slot(2, 2)
                        act.activation(alpha[:, a4:a4 + 1], nmax[:, 1 - p:2 - p], ACT.Exp, bias=nmax[:, p:p + 1], scale=-1.0)
                        if S.has(4):
                            act.wait_ge(ekT_ps, S.upto(4))
                        act.activation(ek[:, p, :], k_b[:], ACT.Exp, bias=nmax[:, p:p + 1],
                                       accum_out=zc[:, a4:a4 + 1]).then_inc(ek_sb, 1)
                    if S.has(1):
                        act.wait_ge(xh_ps, S.upto(1))
                        if S.has(3):
                            act.wait_ge(q_ps, S.upto(3))
                        act.copy(xh[:, S.slot(1, 2), :], xh_b[:]).then_inc(xh_sb, 1)
                    if S.has(2):
                        act.wait_ge(q_sub, S.upto(2))
                        act.activation(qs[:, S.slot(2, 4), :], qs[:, S.slot(2, 4), :], ACT.Exp).then_inc(q_exp, 1)
                    if S.has(0):
                        act.wait_ge(stat, S.upto(0))
                        if S.has(4):
                            act.wait_ge(g_ps, S.upto(4))
                        p = S.slot(0, 2)
                        for t in range(TL):
                            i = act.activation(xhT[:, S.slot(0, 4), t, :], xT_b[p][:, t * C:(t + 1) * C], ACT.Identity,
                                               bias=nmr[:, p, t:t + 1], scale=rstd[:, p, t:t + 1])
                        i.then_inc(ln, 1)
                    if S.has(4):
                        act.wait_ge(qh_ps, S.upto(4))
                        if S.has(6):
                            act.wait_ge(q_kept[S.slot(6, 2)], 16 * S.in_slot(6, 2))
                        act.copy(qh[:, S.slot(4, 2), :], tr_b[:]).then_inc(qh_sb, 1)

                image(act, b, step, A1_DEPTH)

                act.wait_ge(gT_ps, b + 1)
                act.copy(GT[:], tr_b[:, 0:C]).then_inc(gT_sb, 1)

                def step2(S):
                    if S.has(1):
                        act.wait_ge(o_rstd, S.upto(1))
                        if S.has(3):
                            act.wait_ge(on_ps, S.upto(3))
                        p = S.slot(1, 2)
                        for t in range(TL):
                            i = act.activation(onT[:, p, t * C:(t + 1) * C], o_b[p][:, t * C:(t + 1) * C], ACT.Copy,
                                               scale=orstd[:, p, t:t + 1])
                        i.then_inc(o_nrm, 1)
                    if S.has(0):
                        act.wait_ge(o_ps, S.upto(0))
                        if S.has(2):
                            act.wait_ge(o_var, S.upto(2))
                        p = S.slot(0, 2)
                        for t in range(TL):
                            i = act.activation(sq[:, p, t * C:(t + 1) * C], o_b[p][:, t * C:(t + 1) * C], ACT.Square, accum_out=ssq[:, p, t:t + 1])
                        i.then_inc(o_sq, 1)
                    if S.has(5):
                        act.wait_ge(th_ps, S.upto(5))
                        if S.has(7):
                            act.wait_ge(th_st[S.slot(7, 2)], 16 * S.in_slot(7, 2))
                        act.copy(tho[:, S.slot(5, 2), :], th_b[:]).then_inc(th_sb, 1)

                image(act, b, step2, A2_DEPTH + 1)

            scan_scalar(act)

        @block.gpsimd
        def _(pool):
            pool.memset(minus_half[:], -0.5)
            pool.memset(ident[:], 0.0).then_inc(setup_pool, 1)
            pool.wait_ge(setup_pool, 1)
            pool.affine_select(out=ident[:], in_=ident[:], compare_op=ALU.not_equal, fill=1.0, base=0,
                               pattern=[[-1, C]], channel_multiplier=1).then_inc(ident_ok, 1)
            with pool.Fori(0, B) as b:
                def step(S):
                    if S.has(4):
                        pool.wait_ge(q_rec, S.upto(4))
                        if S.has(6):
                            pool.wait_ge(qh_ps, S.upto(6))
                        pool.tensor_tensor(qhT[:, S.slot(4, 2), :].rearrange("q (h d) -> q h d", d=DH),
                                           qs[:, S.slot(4, 4), :].rearrange("q (h d) -> q h d", d=DH),
                                           q_inv[:, S.slot(4, 2), :].unsqueeze(2).to_broadcast([C, TL * HEADS, DH]),
                                           ALU.mult).then_inc(q_nrm, 1)
                    if S.has(0):
                        p = S.slot(0, 2)
                        pool.wait_ge(x_mv, S.upto(0))
                        settle(pool)
                        pool.tensor_scalar(veps[:, 0, :], mv[:, p, :, 1], 1e-6, None, ALU.add).then_inc(x_var, 1)
                        if S.has(2):
                            pool.wait_ge(ln, S.upto(2))
                        pool.wait_ge(x_var, S.upto(0))
                        pool.tensor_tensor(rstd[:, p, :], veps[:, 0, :], minus_half[:], ALU.pow).then_inc(x_rstd, 1)
                        pool.wait_ge(x_rstd, S.upto(0))
                        pool.tensor_tensor(mr[:], mv[:, p, :, 0], rstd[:, p, :], ALU.mult).then_inc(x_mr, 1)
                        pool.wait_ge(x_mr, S.upto(0))
                        settle(pool)
                        pool.tensor_scalar(nmr[:, p, :], mr[:], -1.0, None, ALU.mult).then_inc(stat, 1)

                image(pool, b, step, A1_DEPTH)

                def step2(S):
                    if S.has(0):
                        p = S.slot(0, 2)
                        pool.wait_ge(o_sq, S.upto(0))
                        if S.has(1):
                            pool.wait_ge(o_rstd, S.upto(1))
                        settle(pool)
                        pool.tensor_scalar(veps[:, 1, :], ssq[:, p, :], 1.0 / C, 1e-5, ALU.mult, ALU.add).then_inc(o_var, 1)
                        if S.has(2):
                            pool.wait_ge(o_nrm, S.upto(2))
                        pool.wait_ge(o_var, S.upto(0))
                        pool.tensor_tensor(orstd[:, p, :], veps[:, 1, :], minus_half[:], ALU.pow).then_inc(o_rstd, 1)
                    if S.has(3):
                        p = S.slot(3, 2)
                        pool.wait_ge(s_mv, S.upto(3))
                        if S.has(4):
                            pool.wait_ge(s_rstd, S.upto(4))
                        settle(pool)
                        pool.tensor_scalar(veps[:, 2, :], smv[:, p, :, 1], 1e-5, None, ALU.add).then_inc(s_var, 1)
                        if S.has(5):
                            pool.wait_ge(thT_sb, S.upto(5))
                        pool.wait_ge(s_var, S.upto(3))
                        pool.tensor_tensor(srstd[:, p, :], veps[:, 2, :], minus_half[:], ALU.pow).then_inc(s_rstd, 1)

                image(pool, b, step2, A2_DEPTH)

            pool.wait_ge(bn_var, 1)
            pool.tensor_scalar(small[:, 13:14], small[:, 9:10], 1e-5, None, ALU.add).then_inc(bn_veps, 1)
            pool.wait_ge(bn_veps, 1)
            pool.tensor_tensor(small[:, 10:11], small[:, 13:14], minus_half[:, 0:1], ALU.pow).then_inc(bn_rstd, 1)

        @block.vector
        def _(dve):
            step_n = [0]

            def chain(ins):
                step_n[0] += 1
                ins.then_inc(dve_chain, 1)
                dve.wait_ge(dve_chain, step_n[0])

            chain(dve.memset(head_mask[:], 0.0))
            for h in range(HEADS):
                dve.memset(head_mask[h * DH:(h + 1) * DH, h * DH:(h + 1) * DH], 1.0)
            dve.memset(zeros[:], 0.0)
            chain(dve.memset(thT[:, :, :, C:C + 1], 1.0))
            dve.wait_ge(w_in, 8 * 16)
            chain(dve.tensor_reduce(small[:, 3:4], b_rows[:], AX, ALU.add))
            chain(dve.tensor_scalar(small[:, 4:5], small[:, 3:4], 1.0 / C, None, ALU.mult))
            chain(dve.tensor_scalar(bias_rows[:], b_rows[:], small[:, 4:5], 1.0 / HEADS, ALU.subtract, ALU.mult))
            dve.wait_ge(wT_sb, 6)
            chain(dve.tensor_reduce(small[:, 1:2], WoT[:], AX, ALU.add))
            chain(dve.tensor_scalar(small[:, 2:3], small[:, 1:2], 1.0 / C, None, ALU.mult))
            chain(dve.tensor_scalar(WoT[:], WoT[:], small[:, 2:3], None, ALU.subtract))
            dve.wait_ge(wT_ps, 7)
            dve.tensor_reduce(small[:, 0:1], bank[3][:, 0:C], AX, ALU.add, apply_absolute_value=True).then_inc(cert, 1)
            dve.wait_ge(wT_ps, 8)
            chain(dve.tensor_reduce(cert_row[:, 0:1], bank[3][0:1, C:2 * C], AX, ALU.max))
            chain(dve.tensor_scalar(cert_row[:, 1:2], cert_row[:, 0:1], CONTRACT, None, ALU.is_le))
            dve.tensor_scalar(n_sweeps[:], cert_row[:, 1:2], float(1 - J), float(J), ALU.mult, ALU.add).then_inc(setup, 1)

            with dve.Fori(0, B) as b:
                dve.memset(nmax[:, 1:2], 3e38).then_inc(img_init, 1)
                dve.memset(Z[:], 0.0).then_inc(img_init, 1)
                dve.memset(G[:], 0.0).then_inc(img_init, 1)

                def step(S):
                    if S.has(0):
                        p = S.slot(0, 2)
                        dve.wait_ge(xT_ps, S.upto(0))
                        if S.has(1):
                            dve.wait_ge(x_mv, S.upto(1))
                        for t in range(TL):
                            i = dve.bn_stats(bn6[:, t, :], xT_b[p][:, t * C:(t + 1) * C])
                        i.then_inc(x_bn, 1)
                        if S.has(2):
                            dve.wait_ge(stat, S.upto(2))
                        dve.wait_ge(x_bn, S.upto(0))
                        settle(dve)
                        for t in range(TL):
                            i = dve.bn_aggr(mv[:, p, t, :], bn6[:, t, :])
                        i.then_inc(x_mv, 1)
                    if S.has(2):
                        p = S.slot(2, 2)
                        dve.wait_ge(k_ps, S.upto(2))
                        if S.has(3):
                            dve.wait_ge(k_max, S.upto(3))
                        dve.tensor_reduce(ncmax[:], k_b[:], AX, ALU.max, negate=True).then_inc(kc_max, 1)
                        dve.wait_ge(kc_max, S.upto(2))
                        if S.has(3):
                            dve.wait_ge(ek_sb, S.upto(3))
                        else:
                            dve.wait_ge(img_init, 3 * b + 3)
                        dve.tensor_tensor(nmax[:, p:p + 1], nmax[:, 1 - p:2 - p], ncmax[:], ALU.min).then_inc(k_max, 1)
                        dve.wait_ge(q_ps, S.upto(2))
                        if S.has(3):
                            dve.wait_ge(q_sub, S.upto(3))
                        qv = q_b[:].rearrange("q (h d) -> q h d", d=DH)
                        dve.tensor_reduce(q_mx[:], qv, AX, ALU.max).then_inc(q_max, 1)
                    if S.has(3):
                        dve.wait_ge(q_exp, S.upto(3))
                        if S.has(4):
                            dve.wait_ge(q_rec, S.upto(4))
                        dve.tensor_reduce(q_sum[:], qs[:, S.slot(3, 4), :].rearrange("q (h d) -> q h d", d=DH), AX, ALU.add).then_inc(q_tot, 1)
                    if S.has(2):
                        dve.wait_ge(q_max, S.upto(2))
                        if S.has(6):
                            dve.wait_ge(q_nrm, S.upto(6))
                        dve.tensor_tensor(qs[:, S.slot(2, 4), :].rearrange("q (h d) -> q h d", d=DH), qv,
                                          q_mx[:].unsqueeze(2).to_broadcast([C, TL * HEADS, DH]), ALU.subtract).then_inc(q_sub, 1)
                    if S.has(3):
                        dve.wait_ge(q_tot, S.upto(3))
                        if S.has(5):
                            dve.wait_ge(q_nrm, S.upto(5))
                        dve.reciprocal(q_inv[:, S.slot(3, 2), :], q_sum[:]).then_inc(q_rec, 1)
                    if S.has(4):
                        a4 = S.slot(4, 4)
                        dve.wait_ge(ek_sb, S.upto(4))
                        if S.has(5):
                            dve.wait_ge(z_upd, S.upto(5))
                        dve.scalar_tensor_tensor(Z[:], Z[:], alpha[:, a4:a4 + 1], zc[:, a4:a4 + 1],
                                                 ALU.mult, ALU.add).then_inc(z_upd, 1)
                        dve.wait_ge(g_ps, S.upto(4))
                        if S.has(5):
                            dve.wait_ge(g_upd, S.upto(5))
                        dve.scalar_tensor_tensor(G[:], G[:], alpha[:, a4:a4 + 1], g_b[:, 0:C],
                                                 ALU.mult, ALU.add).then_inc(g_upd, 1)

                image(dve, b, step, A1_DEPTH)

                dve.wait_ge(z_upd, (b + 1) * NC)
                dve.reciprocal(small[:, 5:6], Z[:]).then_inc(img_rz, 1)
                dve.wait_ge(img_rz, b + 1)
                dve.wait_ge(g_upd, (b + 1) * NC)
                dve.tensor_scalar(Gs[:], G[:], small[:, 5:6], DH ** -0.5 / N, ALU.mult, ALU.mult).then_inc(gs_sb, 1)
                dve.wait_ge(ctx_ps, b + 1)
                dve.tensor_tensor(ctxT[:], tr_b[:, C:2 * C], head_mask[:], ALU.mult).then_inc(ctx_sb, 1)
                dve.wait_ge(m_ps, b + 1)
                dve.tensor_tensor(MT[:], g_b[:, 0:C], bias_rows[:], ALU.add).then_inc(m_sb, 1)

                def step2(S):
                    if S.has(2):
                        u = S.slot(2, 4)
                        dve.wait_ge(on_ps, S.upto(2))
                        dve.wait_ge(x2_in[u], 16 * S.in_slot(2, 4))
                        if S.has(6):
                            dve.wait_ge(x1T_ps, S.upto(6))
                            dve.wait_ge(x1_st[u], 16 * S.in_slot(6, 4))
                        dve.scalar_tensor_tensor(x1o[:, u, :], on_b[:], cols_in[:, 2:3], x2in[:, u, :],
                                                 ALU.mult, ALU.add).then_inc(x1_sb, 1)
                    if S.has(3):
                        p = S.slot(3, 2)
                        dve.wait_ge(x1T_ps, S.upto(3))
                        if S.has(4):
                            dve.wait_ge(s_mv, S.upto(4))
                        for t in range(TL):
                            i = dve.bn_stats(s6[:, t, :], x1T_b[p][:, t * C:(t + 1) * C])
                        i.then_inc(s_bn, 1)
                    if S.has(4):
                        p = S.slot(4, 2)
                        dve.wait_ge(s_rstd, S.upto(4))
                        if S.has(6):
                            dve.wait_ge(th_ps, S.upto(6))
                        for t in range(TL):
                            i = dve.tensor_scalar(thT[:, p, t, 0:C], x1T_b[p][:, t * C:(t + 1) * C], smv[:, p, t, 0:1],
                                                  srstd[:, p, t:t + 1], ALU.subtract, ALU.mult)
                        i.then_inc(thT_sb, 1)
                    if S.has(3):
                        p = S.slot(3, 2)
                        if S.has(5):
                            dve.wait_ge(thT_sb, S.upto(5))
                        dve.wait_ge(s_bn, S.upto(3))
                        settle(dve)
                        for t in range(TL):
                            i = dve.bn_aggr(smv[:, p, t, :], s6[:, t, :])
                        i.then_inc(s_mv, 1)

                image(dve, b, step2, A2_DEPTH)

            dve.wait_ge(gram_ps, B * NC)
            dve.tensor_scalar(cov[:], gram[:, 0:C + 1], 1.0 / TOK, None, ALU.mult).then_inc(bn_c, 1)
            dve.wait_ge(bn_ps, 1)
            chain(dve.tensor_tensor(tmp[:], bank[1][:, 0:C], W_in[:], ALU.mult))
            chain(dve.tensor_reduce(small[:, 6:7], tmp[:], AX, ALU.add))
            chain(dve.tensor_copy(small[:, 7:8], bank[1][:, C:C + 1]))
            chain(dve.tensor_tensor(small[:, 8:9], small[:, 7:8], small[:, 7:8], ALU.mult))
            dve.tensor_tensor(small[:, 9:10], small[:, 6:7], small[:, 8:9], ALU.subtract).then_inc(bn_var, 1)
            dve.wait_ge(bn_rstd, 1)
            chain(dve.tensor_tensor(small[:, 11:12], small[:, 10:11], cols_in[:, 0:1], ALU.mult))
            dve.tensor_scalar(Wz[:], W_in[:], small[:, 11:12], None, ALU.mult).then_inc(bn_w, 1)
            chain(dve.tensor_tensor(small[:, 12:13], small[:, 7:8], small[:, 11:12], ALU.mult))
            chain(dve.tensor_tensor(zbias[:], cols_in[:, 1:2], small[:, 12:13], ALU.subtract))
            dve.wait_ge(bn_wps, 1)
            dve.tensor_copy(WzT[:], bank[2][:, 0:C]).then_inc(bn_done, 1)
            scan_vector(dve)

_INS = ["x", "L0_conv_w_qkv", "L0_conv_w_out", "L0_conv_g", "L0_conv_b_out", "L0_ffn_W", "L0_ffn_V", "L0_ffn_gamma", "L0_ffn_beta"]


def program(nc, shapes):
    t = {n: nc.dram_tensor(f"in_{n}", s, F32, kind="ExternalInput").ap() for n, s in shapes.items()}
    out = nc.dram_tensor("out", shapes["x"], F32, kind="ExternalOutput").ap()
    build(nc, t["x"].rearrange("b c h w -> b c (h w)"), t["L0_conv_w_qkv"], t["L0_conv_w_out"], t["L0_conv_b_out"],
          t["L0_conv_g"], t["L0_ffn_W"], t["L0_ffn_V"], t["L0_ffn_gamma"], t["L0_ffn_beta"],
          out.rearrange("b c h w -> b c (h w)"))


def kernel(**inputs):
    import concourse.bacc as bacc
    from concourse.bass_utils import run_bass_kernel_spmd

    nc = bacc.Bacc("TRN2", target_bir_lowering=False, num_devices=1)
    arrays = {n: np.ascontiguousarray(inputs[n]) for n in _INS}
    program(nc, {n: arrays[n].shape for n in _INS})
    r = run_bass_kernel_spmd(nc, [{f"in_{n}": arrays[n] for n in _INS}], core_ids=[0])
    return r.results[0]["out"]
```

```python
import numpy as np
import concourse.bass as bass
from concourse import mybir
from contextlib import ExitStack

F32 = mybir.dt.float32
BF16 = mybir.dt.bfloat16
I32 = mybir.dt.int32
ALU = mybir.AluOpType
ACT = mybir.ActivationFunctionType
AX = mybir.AxisListType.X

C = 128
HEADS = 4
DH = C // HEADS
CH = 512
TL = CH // 128
SEG = 1024
SG = 4
ST = CH // SG
T = 64
GS = 4
NG = T // GS
RING = 2
CONTRACT = 1.01
HEAD = 8


def build(nc, x, w_qkv, w_out, b_out, g, W, V, gamma, beta, out):
    B, _, N = x.shape
    NC = N // CH
    J = N // SEG
    NB = SEG // T
    COLS = B * J
    CC = COLS // 2
    TOK = B * N
    assert J % SG == 0 and SEG // ST == 8 and ST == 2 * T and NB % 2 == 0 and CC * GS <= 512
    assert NC > HEAD and NC % 8 == 0 and B % 2 == 0 and NC * TL <= C and B * C <= 4 * 512

    x1_s = nc.dram_tensor("x1_scratch", (NB, C, COLS, T), F32).ap()
    r_s = nc.dram_tensor("r_scratch", (3, NB, COLS, T), BF16).ap()

    x_v = x.rearrange("b c (m s n) -> b c m s n", s=SG, n=SEG)

    with ExitStack() as ctx:
        def sem(name):
            return ctx.enter_context(nc.semaphore(name))

        def sb(name, shape, dt=F32, stack=ctx):
            return stack.enter_context(nc.sbuf_tensor(name, shape, dt))

        bank = [ctx.enter_context(nc.psum_tensor(f"bank{i}", [C, 512], F32)) for i in range(8)]

        ident = sb("ident", [C, C])
        VT = sb("VT", [C, C])
        WzT = sb("WzT", [C, C])
        zbias = sb("zbias", [C, 1])
        r_all = sb("r_all", [C, TOK // C])
        ones = sb("ones", [64, C], BF16)
        y = [sb(f"y{c}", [C, RING, GS, CC]) for c in range(2)]
        y_start = [sb(f"y_start{c}", [C, CC]) for c in range(2)]
        n_sweeps = sb("n_sweeps", [1, 1], I32)

        w_in, ident_ok = sem("w_in"), sem("ident_ok")
        wT_ps, cert = sem("wT_ps"), sem("cert")
        wT_sb, setup, setup_pool, dve_chain = (sem(s) for s in ("wT_sb", "setup", "setup_pool", "dve_chain"))
        x_in = [sem(f"x_in{i}") for i in range(4)]
        xT_ps, x_bn, x_mv, x_var, x_rstd, x_mr, stat, ln = (
            sem(s) for s in ("xT_ps", "x_bn", "x_mv", "x_var", "x_rstd", "x_mr", "stat", "ln"))
        xh_ps, xh_sb, k_ps, kc_max, k_max, ek_sb, ekT_ps, ekT_sb, g_ps, z_upd, g_upd = (
            sem(s) for s in ("xh_ps", "xh_sb", "k_ps", "kc_max", "k_max", "ek_sb", "ekT_ps", "ekT_sb", "g_ps", "z_upd", "g_upd"))
        q_ps, q_max, q_sub, q_exp, q_tot, q_rec, q_nrm, qh_ps, qh_sb = (
            sem(s) for s in ("q_ps", "q_max", "q_sub", "q_exp", "q_tot", "q_rec", "q_nrm", "qh_ps", "qh_sb"))
        img_init, img_rz, gs_sb, gT_ps, gT_sb, ctx_ps, ctx_sb, m_ps, m_sb = (
            sem(s) for s in ("img_init", "img_rz", "gs_sb", "gT_ps", "gT_sb", "ctx_ps", "ctx_sb", "m_ps", "m_sb"))
        x2_in = [sem(f"x2_in{i}") for i in range(4)]
        q_in = [sem(f"q_in{i}") for i in range(4)]
        o_ps, o_sq, o_var, o_rstd, o_nrm, on_ps, x1_sb, x1T_ps, s_bn, s_mv, s_var, s_rstd, thT_sb, gram_ps, s_nmr, s_kept, thT_act = (
            sem(s) for s in ("o_ps", "o_sq", "o_var", "o_rstd", "o_nrm", "on_ps", "x1_sb", "x1T_ps", "s_bn", "s_mv", "s_var",
                             "s_rstd", "thT_sb", "gram_ps", "s_nmr", "s_kept", "thT_act"))
        x1_st = [sem(f"x1_st{i}") for i in range(4)]
        r_perm, rT_ps, rT_sb, r_split, r_st = (sem(s) for s in ("r_perm", "rT_ps", "rT_sb", "r_split", "r_st"))
        bn_c, bn_ps, bn_var, bn_veps, bn_rstd, bn_w, bn_wps, bn_done = (
            sem(s) for s in ("bn_c", "bn_ps", "bn_var", "bn_veps", "bn_rstd", "bn_w", "bn_wps", "bn_done"))
        settled = {e.engine: sem(f"settled_{n}") for n, e in (("sp", nc.sync), ("pool", nc.gpsimd), ("dve", nc.vector))}
        r_in = [sem(f"r_in{p}") for p in range(2)]
        x1_in = [sem(f"x1_in{p}") for p in range(2)]
        out_st = [sem(f"out_st{p}") for p in range(2)]
        start_ok = [sem(f"start_ok{c}") for c in range(2)]
        r_ps = [sem(f"r_ps{c}") for c in range(2)]
        th_ok = [sem(f"th_ok{c}") for c in range(2)]
        z_done = [sem(f"z_done{c}") for c in range(2)]
        pre_ps = [sem(f"pre_ps{c}") for c in range(2)]
        y_sb = [sem(f"y_sb{c}") for c in range(2)]
        slot_free = [sem(f"slot_free{c}") for c in range(2)]

        a = ExitStack()

        def sa(name, shape, dt=F32):
            return sb(name, shape, dt, a)

        wqkv_in = sa("wqkv_in", [C, 3, C])
        wout_in = sa("wout_in", [C, C])
        W_in = sa("W_in", [C, C])
        V_in = sa("V_in", [C, C])
        cols_in = sa("cols_in", [C, 3])
        b_rows = sa("b_rows", [C, C])
        WqT, WkT, WvT = sa("WqT", [C, C]), sa("WkT", [C, C]), sa("WvT", [C, C])
        WoT = sa("WoT", [C, C])
        bias_rows = sa("bias_rows", [C, C])
        WT = sa("WT", [C, C])
        head_mask = sa("head_mask", [C, C])
        tmp = sa("tmp", [C, C])
        small = sa("small", [C, 16])
        cert_row = sa("cert_row", [1, 4])
        minus_half = sa("minus_half", [C, TL])
        veps = sa("veps", [C, 3, TL])
        zeros = sa("zeros", [C, C + 1])
        rP = sa("rP", [C, B * NC * TL])
        rT = sa("rT", [C, B * C])
        rS = sa("rS", [C, 3, B * C], BF16)
        cov = sa("cov", [C, C + 1])
        Wz = sa("Wz", [C, C])


        xin = sa("xin", [C, 4, CH])
        bn6 = sa("bn6", [C, TL, 6])
        mv = sa("mv", [C, 2, TL, 2])
        rstd = sa("rstd", [C, 2, TL])
        nmr = sa("nmr", [C, 2, TL])
        mr = sa("mr", [C, TL])
        xhT = sa("xhT", [C, 4, TL, C])
        xh = sa("xh", [C, 2, CH])
        nmax = sa("nmax", [C, 2])
        ncmax = sa("ncmax", [C, 1])
        alpha = sa("alpha", [C, 4])
        zc = sa("zc", [C, 4])
        Z = sa("Z", [C, 1])
        G = sa("G", [C, C])
        Gs = sa("Gs", [C, C])
        GT = sa("GT", [C, C])
        ctxT = sa("ctxT", [C, C])
        MT = sa("MT", [C, C])
        ek = sa("ek", [C, 2, CH])
        ekT = sa("ekT", [C, 2, CH])
        q_mx = sa("q_mx", [C, TL * HEADS])
        qs = sa("qs", [C, 4, CH])
        q_sum = sa("q_sum", [C, TL * HEADS])
        q_inv = sa("q_inv", [C, 2, TL * HEADS])
        qhT = sa("qhT", [C, 2, CH])
        q_image = sa("q_image", [C, N])

        x2in = sa("x2in", [C, 4, CH])
        qin = sa("qin", [C, 4, CH])
        sq = sa("sq", [C, 2, CH])
        ssq = sa("ssq", [C, 2, TL])
        orstd = sa("orstd", [C, 2, TL])
        onT = sa("onT", [C, 2, CH])
        s6 = sa("s6", [C, TL, 6])
        smv = sa("smv", [C, 2, TL, 2])
        srstd = sa("srstd", [C, 2, TL])
        thT = sa("thT", [C, 2, TL, C + 1])
        x1o = sa("x1o", [C, 4, CH])
        snmr = sa("snmr", [C, 2, TL])

        gram = bank[0]
        xT_b = [bank[1], bank[2]]
        xh_b, k_b, q_b, tr_b, ekT_b = bank[3], bank[4], bank[5], bank[6], bank[7]
        o_b, on_b = [bank[1], bank[2]], bank[3]
        x1T_b = [[bank[4], bank[5]], [bank[6], bank[7]]]

        def settle(eng):
            eng.sem_inc(settled[eng.engine], 1)

        class Step:
            def __init__(self, b, s, k=None):
                self.b, self.s, self.k = b, s, k

            def has(self, lag):
                if self.k is None:
                    return 0 <= self.s - lag < NC
                assert self.s >= lag
                return True

            def local(self, lag):
                return self.s - lag if self.k is None else self.k * 4 + (self.s - lag)

            def later_image(self):
                return not (isinstance(self.b, int) and self.b == 0)

            def upto(self, lag):
                return self.b * NC + self.local(lag) + 1

            def slot(self, lag, ring):
                return (self.s - lag) % ring

            def in_slot(self, lag, ring):
                c = (self.s - lag) // ring + 1
                return self.b * (NC // ring) + (c if self.k is None else c + self.k * (4 // ring))

        A1_DEPTH, A2_DEPTH = 4, 5
        EARLY = A2_DEPTH - 1

        def images(eng, a1, mixer, a2):
            def loop(b, step):
                with eng.Fori(0, (NC - HEAD) // 4) as k:
                    for s in range(HEAD, HEAD + 4):
                        step(Step(b, s, k))

            def one(b, last):
                for s in range(EARLY, HEAD):
                    a1(Step(b, s))
                loop(b, a1)
                for s in range(NC, NC + A1_DEPTH):
                    a1(Step(b, s))
                mixer(b)
                for s in range(HEAD):
                    a2(Step(b, s))
                loop(b, a2)
                for d in range(A2_DEPTH):
                    a2(Step(b, NC + d))
                    if d >= 1 and not last:
                        a1(Step(b + 1, d - 1))

            for s in range(EARLY):
                a1(Step(0, s))
            with eng.Fori(0, B - 1) as b:
                one(b, False)
            one(B - 1, True)

        def store_r(eng, half):
            dst = r_s.rearrange("e k (b m s) t -> e b m k (s t)", b=B, s=2)
            for e in range(3):
                eng.wait_ge(r_split, e + 1)
                for b in range(half, B, 2):
                    eng.dma_start(dst[e, b], rS[0:NC * TL, e, b * C:(b + 1) * C]).then_inc(r_st, 16)

        a.close()
        x1_t = [sb("x1_t0", [C, COLS, T])]
        if COLS * T < 10240:
            sb("gap", [C, 10240 - COLS * T])
        x1_t.append(sb("x1_t1", [C, COLS, T]))
        r_t = sb("r_t", [64, COLS, T], BF16)
        r_rows = [slice(32 * p, 32 * p + 3) for p in range(2)]
        th_t = [sb(f"th_t{c}", [C, 2, GS, CC]) for c in range(2)]
        z_b = [[bank[1], bank[2]], [bank[3], bank[4]]]
        r_b = [bank[5], bank[6]]
        out_v = out.rearrange("b c (j k t) -> k c b j t", k=NB, t=T)
        SWEEP = NB * NG
        zero_col = [yb[:].rearrange("p (b j) -> p b j", j=J) for yb in y_start]


        def load_x1(sp, blk, p):
            sp.dma_start(x1_t[p][:], x1_s[bass.ds(blk, 1)].rearrange("o c s t -> (o c) s t")).then_inc(x1_in[p], 16)

        def scan_dma(sp):
            def load_r(blk, p):
                sp.dma_start(r_t[r_rows[p]], r_s[:, bass.ds(blk, 1)].rearrange("e o s t -> e (o s) t")).then_inc(r_in[p], 16)

            sp.wait_ge(bn_done, 1)
            load_r(NB - 1, 1)
            sweeps = sp.value_load(n_sweeps[0:1, 0:1], min_val=1, max_val=J)
            with sp.Fori(0, sweeps) as w:
                def loads(blk, p, used, stored):
                    if used is not None:
                        for c in range(2):
                            sp.wait_ge(th_ok[c], used)
                            settle(sp)
                    load_r(blk, p)
                    if stored is not None:
                        sp.wait_ge(out_st[p], stored)
                        settle(sp)
                    load_x1(sp, blk, p)

                def store(blk, p):
                    for c in range(2):
                        sp.wait_ge(slot_free[c], w * SWEEP + blk * NG + NG + RING)
                        settle(sp)
                    src = x1_t[p][:].rearrange("c (b j) t -> c b j t", j=J)
                    for b in range(B):
                        sp.dma_start(out_v[bass.ds(blk, 1), :, b].rearrange("o c j t -> (o c) j t"), src[:, b]).then_inc(out_st[p], 16)

                stores = w * (NB // 2)
                loads(0, 0, None, None)
                loads(1, 1, w * SWEEP + NG, None)
                with sp.Fori(0, (NB - 2) // 2) as k:
                    for p in range(2):
                        store(2 * k + p, p)
                        loads(2 * k + 2 + p, p, w * SWEEP + (2 * k + p + 2) * NG, (stores + k + 1) * 16 * B)
                for p in range(2):
                    store(NB - 2 + p, p)
                for p in range(2):
                    sp.wait_ge(out_st[p], (stores + NB // 2) * 16 * B)
                    settle(sp)

        def scan_tensor(pe):
            def block_steps(group, p, loaded, start, ahead):
                def r_piece(g, c):
                    q, h = (p, g) if g < NG else (1 - p, g - NG)
                    if h == 0 and c == 0:
                        pe.wait_ge(r_in[q], 16 * (loaded if q == p else loaded + 1 - p))
                    if not isinstance(group, int) or group + g > 0:
                        pe.wait_ge(th_ok[c], group + g)
                    pe.matmul(r_b[c][:, 0:GS * CC], ones[r_rows[q]], r_t[r_rows[q], c * CC:(c + 1) * CC, h * GS:(h + 1) * GS]
                              .rearrange("e s u -> e u s"), start=True, stop=True).then_inc(r_ps[c], 1)

                def z_piece(g, u, c):
                    if u == 0:
                        pe.wait_ge(th_ok[c], group + g + 1)
                    i = pe.matmul(z_b[c][g % 2][:, u * CC:(u + 1) * CC], WzT[:], th_t[c][:, g % 2, u, :],
                                  start=(u == 0), stop=False, skip_group_check=True)
                    if u == GS - 1:
                        i.then_inc(z_done[c], 1)

                if start is not None:
                    for g in range(2):
                        for c in range(2):
                            r_piece(g, c)
                        if g == 0:
                            for u in range(GS):
                                for c in range(2):
                                    z_piece(0, u, c)
                for g in range(NG):
                    for u in range(GS):
                        for c in range(2):
                            if g == 0 and u == 0 and start is not None:
                                pe.wait_ge(start_ok[c], start)
                                last = y_start[c][:]
                            else:
                                pe.wait_ge(y_sb[c], (group + g) * GS + u)
                                last = y[c][:, (g if u else g - 1) % RING, (u - 1) % GS, :]
                            pe.matmul(z_b[c][g % 2][:, u * CC:(u + 1) * CC], VT[:], last, start=False, stop=(u == GS - 1),
                                      skip_group_check=True).then_inc(pre_ps[c], 1)
                            if g + 1 < NG:
                                z_piece(g + 1, u, c)
                            if u == 1 and (g + 2 < NG or ahead and g + 2 == NG):
                                r_piece(g + 2, c)
                if ahead:
                    for u in range(GS):
                        for c in range(2):
                            z_piece(NG, u, c)
                    for c in range(2):
                        r_piece(NG + 1, c)

            block_steps(0, 1, 1, 1, False)
            sweeps = pe.value_load(n_sweeps[0:1, 0:1], min_val=1, max_val=J)
            with pe.Fori(0, sweeps) as w:
                half = w * (NB // 2)
                first = w * SWEEP + NG
                block_steps(first, 0, half + 1, w + 2, True)
                with pe.Fori(0, NB // 2 - 1) as k:
                    for i in range(2):
                        block_steps(first + (2 * k + 1 + i) * NG, 1 - i, half + k + 2, None, True)
                block_steps(first + (NB - 1) * NG, 1, half + NB // 2 + 1, None, False)

        def scan_scalar(act):
            def block_steps(group, used):
                for g in range(NG):
                    for u in range(GS):
                        for c in range(2):
                            act.wait_ge(pre_ps[c], (group + g) * GS + u + 1)
                            if u == 0 and used is not None:
                                act.wait_ge(slot_free[c], used + g + 1)
                            act.activation(y[c][:, g % RING, u, :], z_b[c][g % 2][:, u * CC:(u + 1) * CC], ACT.Sigmoid,
                                           bias=zbias[:]).then_inc(y_sb[c], 1)

            act.wait_ge(bn_done, 1)
            block_steps(0, None)
            sweeps = act.value_load(n_sweeps[0:1, 0:1], min_val=1, max_val=J)
            with act.Fori(0, sweeps) as w:
                with act.Fori(0, NB) as k:
                    block_steps(w * SWEEP + k * NG + NG, w * SWEEP + k * NG)

        def scan_vector(dve):
            def block_steps(group, p, loaded, first, adds, ahead):
                def scale(g, c):
                    q, h = (p, g) if g < NG else (1 - p, g - NG)
                    if h == 0 and c == 0:
                        dve.wait_ge(x1_in[q], 16 * (loaded if q == p else loaded + 1 - p))
                    dve.wait_ge(r_ps[c], group + g + 1)
                    if not isinstance(group, int) or group + g > 1:
                        dve.wait_ge(z_done[c], group + g - 1)
                    dve.tensor_tensor(th_t[c][:, g % 2], x1_t[q][:, c * CC:(c + 1) * CC, h * GS:(h + 1) * GS]
                                      .rearrange("p s u -> p u s"), r_b[c][:, 0:GS * CC].rearrange("p (u s) -> p u s", u=GS),
                                      ALU.mult).then_inc(th_ok[c], 1)
                if first:
                    for g in range(2):
                        for c in range(2):
                            scale(g, c)
                for g in range(NG):
                    if g + 2 < NG or ahead and g == NG - 1:
                        for c in range(2):
                            scale(min(g + 2, NG), c)
                    if adds:
                        for c in range(2):
                            dve.wait_ge(y_sb[c], (group + g + 1) * GS)
                            dst = x1_t[p][:, c * CC:(c + 1) * CC, g * GS:(g + 1) * GS]
                            dve.tensor_tensor(dst, dst, y[c][:, g % RING, :, :].rearrange("p u s -> p s u"),
                                              ALU.add).then_inc(slot_free[c], 1)
                if ahead:
                    for c in range(2):
                        scale(NG + 1, c)

            for c in range(2):
                dve.memset(y_start[c][:], 0.0).then_inc(start_ok[c], 1)
                dve.sem_inc(slot_free[c], RING)
            block_steps(0, 1, 1, True, False, False)
            sweeps = dve.value_load(n_sweeps[0:1, 0:1], min_val=1, max_val=J)
            with dve.Fori(0, sweeps) as w:
                half = w * (NB // 2)
                start = w * SWEEP + NG
                for c in range(2):
                    dve.wait_ge(y_sb[c], start * GS)
                    ends = y[c][:, RING - 1, GS - 1, :].rearrange("p (b j) -> p b j", j=J)
                    dve.tensor_copy(zero_col[c][:, :, 1:J], ends[:, :, 0:J - 1]).then_inc(start_ok[c], 1)
                block_steps(start, 0, half + 1, True, True, True)
                with dve.Fori(0, NB // 2 - 1) as k:
                    for i in range(2):
                        block_steps(start + (2 * k + 1 + i) * NG, 1 - i, half + k + 2, False, True, True)
                block_steps(start + (NB - 1) * NG, 1, half + NB // 2 + 1, False, True, False)

        block = ctx.enter_context(nc.Block())

        @block.sync
        def _(sp):
            sp.dma_start(wqkv_in[:], w_qkv.rearrange("(a p) c -> p a c", p=C)).then_inc(w_in, 16)
            sp.dma_start(wout_in[:], w_out).then_inc(w_in, 16)
            sp.dma_start(W_in[:], W).then_inc(w_in, 16)
            sp.dma_start(V_in[:], V).then_inc(w_in, 16)
            sp.dma_start(cols_in[:, 0:1], gamma.rearrange("(p a) -> p a", a=1)).then_inc(w_in, 16)
            sp.dma_start(cols_in[:, 1:2], beta.rearrange("(p a) -> p a", a=1)).then_inc(w_in, 16)
            sp.dma_start(cols_in[:, 2:3], g.rearrange("(p a) -> p a", a=1)).then_inc(w_in, 16)
            sp.dma_start(b_rows[:], b_out.partition_broadcast(C)).then_inc(w_in, 16)

            def chunk(b, m, i):
                n = i % 8 * ST
                return x_v[b, :, bass.ds(m + i // 8, 1), :, n:n + ST].rearrange("c o s n -> c (o s) n")

            def load_a1(b, m, i):
                sp.dma_start(xin[:, i % 4, :].rearrange("c (s n) -> c s n", n=ST), chunk(b, m, i)).then_inc(x_in[i % 4], 16)

            def load_x2(b, m, i):
                sp.dma_start(x2in[:, i % 4, :].rearrange("c (s n) -> c s n", n=ST), chunk(b, m, i)).then_inc(x2_in[i % 4], 16)

            def load_q(m, i):
                sp.dma_start(qin[:, i % 4, :], q_image[:, bass.ds((8 * m + i) * CH, CH)]).then_inc(q_in[i % 4], 16)

            def store_x1(b, m, i):
                nb = ST // T
                sp.wait_ge(x1_sb, b * NC + 8 * m + i + 1)
                sp.dma_start(x1_s[i * nb:(i + 1) * nb, :, bass.ds(b * J + SG * m, SG), :].rearrange("k c s t -> c k (s t)"),
                             x1o[:, i % 4, :].rearrange("c (k w) -> c k w", k=nb)).then_inc(x1_st[i % 4], 16)

            def one_image(b, first, last):
                E = NC // 8
                L = NC // 4

                def turn1(m, i):
                    sp.wait_ge(xT_ps, b * NC + 8 * m + i + 1)
                    load_a1(b, m, i + 4)

                with sp.Fori(0, E - 1) as m:
                    for i in range(8):
                        turn1(m, i)
                for i in range(4):
                    turn1(E - 1, i)
                for i in range(4):
                    load_x2(b, 0, i)
                if not first:
                    for u in range(4):
                        sp.wait_ge(x1_st[u], b * L * 16)
                        settle(sp)
                sp.wait_ge(qh_sb, (b + 1) * NC)
                settle(sp)
                for i in range(4):
                    load_q(0, i)
                if not last:
                    for i in range(4):
                        load_a1(b + 1, 0, i)

                def turn2(m, i, ahead=True):
                    if ahead:
                        sp.wait_ge(o_ps, b * NC + 8 * m + i + 1)
                        load_q(m, i + 4)
                    store_x1(b, m, i)
                    if ahead:
                        load_x2(b, m, i + 4)

                with sp.Fori(0, E - 1) as m:
                    for i in range(8):
                        turn2(m, i)
                for i in range(8):
                    turn2(E - 1, i, ahead=i < 4)

            for i in range(4):
                load_a1(0, 0, i)
            one_image(0, True, B == 1)
            if B > 2:
                with sp.Fori(1, B - 1) as b:
                    one_image(b, False, False)
            one_image(B - 1, False, True)
            for u in range(4):
                sp.wait_ge(x1_st[u], B * NC * 4)
            sp.wait_ge(gram_ps, B * NC)
            load_x1(sp, NB - 1, 1)
            store_r(sp, 0)
            sp.wait_ge(r_st, B * 3 * 16)
            scan_dma(sp)

        @block.tensor
        def _(pe):
            pe.wait_ge(w_in, 8 * 16)
            pe.wait_ge(ident_ok, 1)
            srcs = [wqkv_in[:, 0, :], wqkv_in[:, 1, :], wqkv_in[:, 2, :], wout_in[:]]
            for i, s in enumerate(srcs):
                pe.transpose(bank[1][:, i * C:(i + 1) * C], s, ident[:]).then_inc(wT_ps, 1)
            for i, s in enumerate([W_in[:], V_in[:]]):
                pe.transpose(bank[2][:, i * C:(i + 1) * C], s, ident[:]).then_inc(wT_ps, 1)
            pe.wait_ge(wT_sb, 6)
            pe.matmul(bank[3][:, 0:C], VT[:], VT[:], start=True, stop=True).then_inc(wT_ps, 1)
            pe.wait_ge(cert, 1)
            pe.transpose(bank[3][0:1, C:2 * C], small[:, 0:1], ident[:]).then_inc(wT_ps, 1)
            pe.matmul(gram[:, 0:C + 1], zeros[:, 0:C], zeros[:], start=True, stop=False, skip_group_check=True)
            pe.wait_ge(setup, 1)

            def step(S):
                if S.has(0):
                    pe.wait_ge(x_in[S.slot(0, 4)], 16 * S.in_slot(0, 4))
                    if S.has(2):
                        pe.wait_ge(ln, S.upto(2))
                    elif S.later_image():
                        pe.wait_ge(o_nrm, S.b * NC)
                    for t in range(TL):
                        i = pe.transpose(xT_b[S.slot(0, 2)][:, t * C:(t + 1) * C], xin[:, S.slot(0, 4), t * C:(t + 1) * C], ident[:])
                    i.then_inc(xT_ps, 1)
                if S.has(2):
                    pe.wait_ge(xh_sb, S.upto(2))
                    if S.has(3):
                        pe.wait_ge(ek_sb, S.upto(3))
                    elif S.later_image():
                        pe.wait_ge(thT_sb, S.b * NC - 1)
                        pe.wait_ge(thT_act, S.b * NC - 1)
                    pe.matmul(k_b[:], WkT[:], xh[:, S.slot(2, 2), :], start=True, stop=True).then_inc(k_ps, 1)
                if S.has(4):
                    pe.wait_ge(q_nrm, S.upto(4))
                    pe.wait_ge(g_upd, S.upto(4))
                    for t in range(TL):
                        i = pe.transpose(tr_b[:, t * C:(t + 1) * C], qhT[:, S.slot(4, 2), t * C:(t + 1) * C], ident[:])
                    i.then_inc(qh_ps, 1)
                if S.has(2):
                    if S.has(3):
                        pe.wait_ge(q_sub, S.upto(3))
                    for t in range(TL):
                        i = pe.matmul(q_b[:, t * C:(t + 1) * C], xh[:, S.slot(2, 2), t * C:(t + 1) * C], WqT[:], start=True, stop=True)
                    i.then_inc(q_ps, 1)
                if S.has(1):
                    pe.wait_ge(ln, S.upto(1))
                    if S.has(2):
                        pe.wait_ge(xh_sb, S.upto(2))
                    elif S.later_image():
                        pe.wait_ge(x1_sb, S.b * NC)
                    for t in range(TL):
                        i = pe.transpose(xh_b[:, t * C:(t + 1) * C], xhT[:, S.slot(1, 4), t, :], ident[:])
                    i.then_inc(xh_ps, 1)
                if S.has(3):
                    pe.wait_ge(ekT_sb, S.upto(3))
                    if S.has(4):
                        pe.wait_ge(qh_sb, S.upto(4))
                    for t in range(TL):
                        i = pe.matmul(tr_b[:, 0:C], ekT[:, S.slot(3, 2), t * C:(t + 1) * C], xhT[:, S.slot(3, 4), t, :],
                                      start=(t == 0), stop=(t == TL - 1))
                    i.then_inc(g_ps, 1)
                if S.has(2):
                    pe.wait_ge(ek_sb, S.upto(2))
                    if S.has(3):
                        pe.wait_ge(ekT_sb, S.upto(3))
                    elif S.later_image():
                        pe.wait_ge(thT_sb, S.b * NC)
                        pe.wait_ge(thT_act, S.b * NC)
                    for t in range(TL):
                        i = pe.transpose(ekT_b[:, t * C:(t + 1) * C], ek[:, S.slot(2, 2), t * C:(t + 1) * C], ident[:])
                    i.then_inc(ekT_ps, 1)

            def mixer(b):
                pe.wait_ge(qh_sb, (b + 1) * NC)
                pe.wait_ge(q_sub, (b + 1) * NC)
                pe.wait_ge(ekT_sb, (b + 1) * NC)
                pe.wait_ge(gs_sb, b + 1)
                pe.transpose(tr_b[:, 0:C], Gs[:], ident[:]).then_inc(gT_ps, 1)
                pe.wait_ge(gT_sb, b + 1)
                pe.matmul(tr_b[:, C:2 * C], WvT[:], GT[:], start=True, stop=True).then_inc(ctx_ps, 1)
                pe.wait_ge(ctx_sb, b + 1)
                pe.matmul(tr_b[:, 0:C], ctxT[:], WoT[:], start=True, stop=True).then_inc(m_ps, 1)
                pe.wait_ge(m_sb, b + 1)

            def step2(S):
                if S.has(0):
                    pe.wait_ge(q_in[S.slot(0, 4)], 16 * S.in_slot(0, 4))
                    if S.has(2):
                        pe.wait_ge(o_nrm, S.upto(2))
                    for t in range(TL):
                        i = pe.matmul(o_b[S.slot(0, 2)][:, t * C:(t + 1) * C], qin[:, S.slot(0, 4), t * C:(t + 1) * C], MT[:],
                                      start=True, stop=True)
                    i.then_inc(o_ps, 1)
                if S.has(2):
                    pe.wait_ge(o_nrm, S.upto(2))
                    if S.has(3):
                        pe.wait_ge(x1_sb, S.upto(3))
                    for t in range(TL):
                        i = pe.transpose(on_b[:, t * C:(t + 1) * C], onT[:, S.slot(2, 2), t * C:(t + 1) * C], ident[:])
                    i.then_inc(on_ps, 1)
                if S.has(3):
                    pe.wait_ge(x1_sb, S.upto(3))
                    if S.has(5):
                        pe.wait_ge(thT_sb, S.upto(5))
                        pe.wait_ge(thT_act, S.upto(5))
                    for t in range(TL):
                        i = pe.transpose(x1T_b[S.slot(3, 2)][t // 2][:, t % 2 * C:(t % 2 + 1) * C], x1o[:, S.slot(3, 4), t * C:(t + 1) * C], ident[:])
                    i.then_inc(x1T_ps, 1)
                if S.has(5):
                    pe.wait_ge(thT_sb, S.upto(5))
                    pe.wait_ge(thT_act, S.upto(5))
                    for t in range(TL):
                        i = pe.matmul(gram[:, 0:C + 1], thT[:, S.slot(5, 2), t, 0:C], thT[:, S.slot(5, 2), t, :], start=False, stop=False,
                                      skip_group_check=True)
                    i.then_inc(gram_ps, 1)

            images(pe, step, mixer, step2)

            for b in range(B):
                if b == 0:
                    pe.wait_ge(r_perm, 2)
                pe.transpose(bank[4 + b // 4][0:NC * TL, b % 4 * C:(b % 4 + 1) * C], rP[:, b * NC * TL:(b + 1) * NC * TL], ident[:]).then_inc(rT_ps, 1)

            pe.wait_ge(bn_c, 1)
            pe.matmul(bank[1][:, 0:C + 1], WT[:], cov[:], start=True, stop=True).then_inc(bn_ps, 1)
            pe.wait_ge(bn_w, 1)
            pe.transpose(bank[2][:, 0:C], Wz[:], ident[:]).then_inc(bn_wps, 1)
            pe.wait_ge(bn_done, 1)
            scan_tensor(pe)

        @block.scalar
        def _(act):
            act.wait_ge(wT_ps, 6)
            for i, d in enumerate([WqT[:], WkT[:], WvT[:], WoT[:]]):
                act.copy(d, bank[1][:, i * C:(i + 1) * C]).then_inc(wT_sb, 1)
            for i, d in enumerate([WT[:], VT[:]]):
                act.copy(d, bank[2][:, i * C:(i + 1) * C]).then_inc(wT_sb, 1)

            def step(S):
                if S.has(1):
                    act.wait_ge(stat, S.upto(1))
                    if S.has(5):
                        act.wait_ge(g_ps, S.upto(5))
                    p = S.slot(1, 2)
                    for t in range(TL):
                        i = act.activation(xhT[:, S.slot(1, 4), t, :], xT_b[p][:, t * C:(t + 1) * C], ACT.Identity,
                                           bias=nmr[:, p, t:t + 1], scale=rstd[:, p, t:t + 1])
                    i.then_inc(ln, 1)
                if S.has(3):
                    act.wait_ge(q_sub, S.upto(3))
                    act.activation(qs[:, S.slot(3, 4), :], qs[:, S.slot(3, 4), :], ACT.Exp).then_inc(q_exp, 1)
                if S.has(3):
                    act.wait_ge(ekT_ps, S.upto(3))
                    if S.has(5):
                        act.wait_ge(g_ps, S.upto(5))
                    act.copy(ekT[:, S.slot(3, 2), :], ekT_b[:]).then_inc(ekT_sb, 1)
                if S.has(4):
                    act.wait_ge(qh_ps, S.upto(4))
                    act.copy(q_image[:, bass.ds(S.local(4) * CH, CH)], tr_b[:]).then_inc(qh_sb, 1)
                if S.has(2):
                    act.wait_ge(k_max, S.upto(2))
                    if S.has(6):
                        act.wait_ge(g_upd, S.upto(6))
                    a4, p = S.slot(2, 4), S.slot(2, 2)
                    act.activation(alpha[:, a4:a4 + 1], nmax[:, 1 - p:2 - p], ACT.Exp, bias=nmax[:, p:p + 1], scale=-1.0)
                    if S.has(4):
                        act.wait_ge(ekT_ps, S.upto(4))
                    act.activation(ek[:, p, :], k_b[:], ACT.Exp, bias=nmax[:, p:p + 1],
                                   accum_out=zc[:, a4:a4 + 1]).then_inc(ek_sb, 1)
                if S.has(1):
                    act.wait_ge(xh_ps, S.upto(1))
                    if S.has(3):
                        act.wait_ge(q_ps, S.upto(3))
                    act.copy(xh[:, S.slot(1, 2), :], xh_b[:]).then_inc(xh_sb, 1)

            def mixer(b):
                act.wait_ge(gT_ps, b + 1)
                act.copy(GT[:], tr_b[:, 0:C]).then_inc(gT_sb, 1)

            def step2(S):
                if S.has(5):
                    p = S.slot(5, 2)
                    act.wait_ge(s_nmr, S.upto(5))
                    if S.has(7):
                        act.wait_ge(gram_ps, S.upto(7))
                    for t in range(TL // 2, TL):
                        i = act.activation(thT[:, p, t, 0:C], x1T_b[p][t // 2][:, t % 2 * C:(t % 2 + 1) * C], ACT.Identity,
                                           bias=snmr[:, p, t:t + 1], scale=srstd[:, p, t:t + 1])
                    i.then_inc(thT_act, 1)
                if S.has(0):
                    act.wait_ge(o_ps, S.upto(0))
                    if S.has(2):
                        act.wait_ge(o_var, S.upto(2))
                    p = S.slot(0, 2)
                    for t in range(TL):
                        i = act.activation(sq[:, p, t * C:(t + 1) * C], o_b[p][:, t * C:(t + 1) * C], ACT.Square, accum_out=ssq[:, p, t:t + 1])
                    i.then_inc(o_sq, 1)
                if S.has(1):
                    act.wait_ge(o_rstd, S.upto(1))
                    if S.has(3):
                        act.wait_ge(on_ps, S.upto(3))
                    p = S.slot(1, 2)
                    for t in range(TL):
                        i = act.activation(onT[:, p, t * C:(t + 1) * C], o_b[p][:, t * C:(t + 1) * C], ACT.Copy,
                                           scale=orstd[:, p, t:t + 1])
                    i.then_inc(o_nrm, 1)

            images(act, step, mixer, step2)

            for k in range((B + 3) // 4):
                act.wait_ge(rT_ps, min(4 * k + 4, B))
                w = (min(4 * k + 4, B) - 4 * k) * C
                act.copy(rT[0:NC * TL, 4 * k * C:4 * k * C + w], bank[4 + k][0:NC * TL, 0:w]).then_inc(rT_sb, 1)
            store_r(act, 1)
            scan_scalar(act)

        @block.gpsimd
        def _(pool):
            pool.memset(minus_half[:], -0.5)
            pool.memset(ident[:], 0.0).then_inc(setup_pool, 1)
            pool.wait_ge(setup_pool, 1)
            pool.affine_select(out=ident[:], in_=ident[:], compare_op=ALU.not_equal, fill=1.0, base=0,
                               pattern=[[-1, C]], channel_multiplier=1).then_inc(ident_ok, 1)
            def step(S):
                if S.has(0):
                    p = S.slot(0, 2)
                    pool.wait_ge(x_mv, S.upto(0))
                    settle(pool)
                    pool.tensor_scalar(veps[:, 0, :], mv[:, p, :, 1], 1e-6, None, ALU.add).then_inc(x_var, 1)
                    if S.has(2):
                        pool.wait_ge(ln, S.upto(2))
                    pool.wait_ge(x_var, S.upto(0))
                    pool.tensor_tensor(rstd[:, p, :], veps[:, 0, :], minus_half[:], ALU.pow).then_inc(x_rstd, 1)
                    pool.wait_ge(x_rstd, S.upto(0))
                    pool.tensor_tensor(mr[:], mv[:, p, :, 0], rstd[:, p, :], ALU.mult).then_inc(x_mr, 1)
                    pool.wait_ge(x_mr, S.upto(0))
                    settle(pool)
                    pool.tensor_scalar(nmr[:, p, :], mr[:], -1.0, None, ALU.mult).then_inc(stat, 1)
                if S.has(3):
                    pool.wait_ge(q_rec, S.upto(3))
                    if S.has(5):
                        pool.wait_ge(qh_ps, S.upto(5))
                    pool.tensor_tensor(qhT[:, S.slot(3, 2), :].rearrange("q (h d) -> q h d", d=DH),
                                       qs[:, S.slot(3, 4), :].rearrange("q (h d) -> q h d", d=DH),
                                       q_inv[:, S.slot(3, 2), :].unsqueeze(2).to_broadcast([C, TL * HEADS, DH]),
                                       ALU.mult).then_inc(q_nrm, 1)

            def mixer(b):
                pass

            def step2(S):
                if S.has(4):
                    p = S.slot(4, 2)
                    pool.wait_ge(s_mv, S.upto(4))
                    if S.has(5):
                        pool.wait_ge(s_rstd, S.upto(5))
                    settle(pool)
                    pool.tensor_scalar(veps[:, 2, :], smv[:, p, :, 1], 1e-5, None, ALU.add).then_inc(s_var, 1)
                    if S.has(6):
                        pool.wait_ge(thT_sb, S.upto(6))
                        pool.wait_ge(thT_act, S.upto(6))
                    pool.wait_ge(s_var, S.upto(4))
                    pool.tensor_tensor(srstd[:, p, :], veps[:, 2, :], minus_half[:], ALU.pow).then_inc(s_rstd, 1)
                if S.has(0):
                    p = S.slot(0, 2)
                    pool.wait_ge(o_sq, S.upto(0))
                    if S.has(1):
                        pool.wait_ge(o_rstd, S.upto(1))
                    settle(pool)
                    pool.tensor_scalar(veps[:, 1, :], ssq[:, p, :], 1.0 / C, 1e-5, ALU.mult, ALU.add).then_inc(o_var, 1)
                    if S.has(2):
                        pool.wait_ge(o_nrm, S.upto(2))
                    pool.wait_ge(o_var, S.upto(0))
                    pool.tensor_tensor(orstd[:, p, :], veps[:, 1, :], minus_half[:], ALU.pow).then_inc(o_rstd, 1)

            images(pool, step, mixer, step2)

            pool.wait_ge(bn_var, 1)
            pool.tensor_scalar(small[:, 13:14], small[:, 9:10], 1e-5, None, ALU.add).then_inc(bn_veps, 1)
            pool.wait_ge(bn_veps, 1)
            pool.tensor_tensor(small[:, 10:11], small[:, 13:14], minus_half[:, 0:1], ALU.pow).then_inc(bn_rstd, 1)

        @block.vector
        def _(dve):
            step_n = [0]

            def chain(ins):
                step_n[0] += 1
                ins.then_inc(dve_chain, 1)
                dve.wait_ge(dve_chain, step_n[0])

            chain(dve.memset(head_mask[:], 0.0))
            for h in range(HEADS):
                dve.memset(head_mask[h * DH:(h + 1) * DH, h * DH:(h + 1) * DH], 1.0)
            dve.memset(zeros[:], 0.0)
            dve.memset(ones[:], 1.0)
            chain(dve.memset(thT[:, :, :, C:C + 1], 1.0))
            dve.wait_ge(w_in, 8 * 16)
            chain(dve.tensor_reduce(small[:, 3:4], b_rows[:], AX, ALU.add))
            chain(dve.tensor_scalar(small[:, 4:5], small[:, 3:4], 1.0 / C, None, ALU.mult))
            chain(dve.tensor_scalar(bias_rows[:], b_rows[:], small[:, 4:5], 1.0 / HEADS, ALU.subtract, ALU.mult))
            dve.wait_ge(wT_sb, 6)
            chain(dve.tensor_reduce(small[:, 1:2], WoT[:], AX, ALU.add))
            chain(dve.tensor_scalar(small[:, 2:3], small[:, 1:2], 1.0 / C, None, ALU.mult))
            chain(dve.tensor_scalar(WoT[:], WoT[:], small[:, 2:3], None, ALU.subtract))
            dve.wait_ge(wT_ps, 7)
            dve.tensor_reduce(small[:, 0:1], bank[3][:, 0:C], AX, ALU.add, apply_absolute_value=True).then_inc(cert, 1)
            dve.wait_ge(wT_ps, 8)
            chain(dve.tensor_reduce(cert_row[:, 0:1], bank[3][0:1, C:2 * C], AX, ALU.max))
            chain(dve.tensor_scalar(cert_row[:, 1:2], cert_row[:, 0:1], CONTRACT, None, ALU.is_le))
            dve.tensor_scalar(n_sweeps[:], cert_row[:, 1:2], float(1 - J), float(J), ALU.mult, ALU.add).then_inc(setup, 1)

            def step(S):
                if S.s == 0 and S.k is None:
                    dve.memset(nmax[:, 1:2], 3e38).then_inc(img_init, 1)
                    dve.memset(Z[:], 0.0).then_inc(img_init, 1)
                    dve.memset(G[:], 0.0).then_inc(img_init, 1)
                if S.has(0):
                    p = S.slot(0, 2)
                    dve.wait_ge(xT_ps, S.upto(0))
                    if S.has(1):
                        dve.wait_ge(x_mv, S.upto(1))
                    for t in range(TL):
                        i = dve.bn_stats(bn6[:, t, :], xT_b[p][:, t * C:(t + 1) * C])
                    i.then_inc(x_bn, 1)
                if S.has(2):
                    p = S.slot(2, 2)
                    dve.wait_ge(k_ps, S.upto(2))
                    if S.has(3):
                        dve.wait_ge(k_max, S.upto(3))
                    dve.tensor_reduce(ncmax[:], k_b[:], AX, ALU.max, negate=True).then_inc(kc_max, 1)
                if S.has(0):
                    p = S.slot(0, 2)
                    if S.has(2):
                        dve.wait_ge(stat, S.upto(2))
                    dve.wait_ge(x_bn, S.upto(0))
                    settle(dve)
                    for t in range(TL):
                        i = dve.bn_aggr(mv[:, p, t, :], bn6[:, t, :])
                    i.then_inc(x_mv, 1)
                if S.has(2):
                    p = S.slot(2, 2)
                    dve.wait_ge(kc_max, S.upto(2))
                    if S.has(3):
                        dve.wait_ge(ek_sb, S.upto(3))
                    else:
                        dve.wait_ge(img_init, 3 * S.b + 3)
                    dve.tensor_tensor(nmax[:, p:p + 1], nmax[:, 1 - p:2 - p], ncmax[:], ALU.min).then_inc(k_max, 1)
                if S.has(3):
                    a4 = S.slot(3, 4)
                    dve.wait_ge(q_exp, S.upto(3))
                    if S.has(4):
                        dve.wait_ge(q_rec, S.upto(4))
                    dve.tensor_reduce(q_sum[:], qs[:, a4, :].rearrange("q (h d) -> q h d", d=DH), AX, ALU.add).then_inc(q_tot, 1)
                    dve.wait_ge(ek_sb, S.upto(3))
                    if S.has(4):
                        dve.wait_ge(z_upd, S.upto(4))
                    dve.scalar_tensor_tensor(Z[:], Z[:], alpha[:, a4:a4 + 1], zc[:, a4:a4 + 1],
                                             ALU.mult, ALU.add).then_inc(z_upd, 1)
                    dve.wait_ge(q_tot, S.upto(3))
                    if S.has(5):
                        dve.wait_ge(q_nrm, S.upto(5))
                    dve.reciprocal(q_inv[:, S.slot(3, 2), :], q_sum[:]).then_inc(q_rec, 1)
                if S.has(2):
                    dve.wait_ge(q_ps, S.upto(2))
                    if S.has(3):
                        dve.wait_ge(q_sub, S.upto(3))
                    qv = q_b[:].rearrange("q (h d) -> q h d", d=DH)
                    dve.tensor_reduce(q_mx[:], qv, AX, ALU.max).then_inc(q_max, 1)
                if S.has(3):
                    dve.wait_ge(g_ps, S.upto(3))
                    if S.has(4):
                        dve.wait_ge(g_upd, S.upto(4))
                    dve.scalar_tensor_tensor(G[:], G[:], alpha[:, a4:a4 + 1], tr_b[:, 0:C],
                                             ALU.mult, ALU.add).then_inc(g_upd, 1)
                if S.has(2):
                    dve.wait_ge(q_max, S.upto(2))
                    if S.has(6):
                        dve.wait_ge(q_nrm, S.upto(6))
                    dve.tensor_tensor(qs[:, S.slot(2, 4), :].rearrange("q (h d) -> q h d", d=DH), qv,
                                      q_mx[:].unsqueeze(2).to_broadcast([C, TL * HEADS, DH]), ALU.subtract).then_inc(q_sub, 1)

            def mixer(b):
                dve.wait_ge(z_upd, (b + 1) * NC)
                dve.reciprocal(small[:, 5:6], Z[:]).then_inc(img_rz, 1)
                dve.wait_ge(img_rz, b + 1)
                dve.wait_ge(g_upd, (b + 1) * NC)
                dve.tensor_scalar(Gs[:], G[:], small[:, 5:6], DH ** -0.5 / N, ALU.mult, ALU.mult).then_inc(gs_sb, 1)
                dve.wait_ge(ctx_ps, b + 1)
                dve.tensor_tensor(ctxT[:], tr_b[:, C:2 * C], head_mask[:], ALU.mult).then_inc(ctx_sb, 1)
                dve.wait_ge(m_ps, b + 1)
                dve.tensor_tensor(MT[:], tr_b[:, 0:C], bias_rows[:], ALU.add).then_inc(m_sb, 1)

            def step2(S):
                if S.has(5):
                    p = S.slot(5, 2)
                    dve.wait_ge(s_rstd, S.upto(5))
                    if S.has(7):
                        dve.wait_ge(gram_ps, S.upto(7))
                    for t in range(TL // 2):
                        i = dve.tensor_scalar(thT[:, p, t, 0:C], x1T_b[p][t // 2][:, t % 2 * C:(t % 2 + 1) * C], smv[:, p, t, 0:1],
                                              srstd[:, p, t:t + 1], ALU.subtract, ALU.mult)
                    i.then_inc(thT_sb, 1)
                if S.has(2):
                    u = S.slot(2, 4)
                    dve.wait_ge(on_ps, S.upto(2))
                    dve.wait_ge(x2_in[u], 16 * S.in_slot(2, 4))
                    if S.has(6):
                        dve.wait_ge(x1T_ps, S.upto(6))
                        dve.wait_ge(x1_st[u], 16 * S.in_slot(6, 4))
                    x1_v = x1o[:, u, :].rearrange("c (k s t) -> c k s t", s=SG, t=T)
                    on_v, x2_v = (a.rearrange("c (s k t) -> c k s t", s=SG, t=T) for a in (on_b[:], x2in[:, u, :]))
                    for k in range(ST // T):
                        i = dve.scalar_tensor_tensor(x1_v[:, k], on_v[:, k], cols_in[:, 2:3], x2_v[:, k],
                                                     ALU.mult, ALU.add)
                    i.then_inc(x1_sb, 1)
                if S.has(3):
                    p = S.slot(3, 2)
                    dve.wait_ge(x1T_ps, S.upto(3))
                    if S.has(4):
                        dve.wait_ge(s_mv, S.upto(4))
                    for t in range(TL):
                        i = dve.bn_stats(s6[:, t, :], x1T_b[p][t // 2][:, t % 2 * C:(t % 2 + 1) * C])
                    i.then_inc(s_bn, 1)
                if S.has(4):
                    q = S.slot(4, 2)
                    dve.wait_ge(s_rstd, S.upto(4))
                    if S.has(6):
                        dve.wait_ge(thT_act, S.upto(6))
                    dve.scalar_tensor_tensor(snmr[:, q, :], smv[:, q, :, 0], -1.0, srstd[:, q, :], ALU.mult, ALU.mult).then_inc(s_nmr, 1)
                    dve.tensor_copy(r_all[:, bass.ds((S.upto(4) - 1) * TL, TL)], srstd[:, q, :]).then_inc(s_kept, 1)
                if S.has(3):
                    p = S.slot(3, 2)
                    if S.has(5):
                        dve.wait_ge(thT_sb, S.upto(5))
                    dve.wait_ge(s_bn, S.upto(3))
                    settle(dve)
                    for t in range(TL):
                        i = dve.bn_aggr(smv[:, p, t, :], s6[:, t, :])
                    i.then_inc(s_mv, 1)

            images(dve, step, mixer, step2)

            R = NC * TL
            dve.wait_ge(s_kept, B * NC)
            r_from = r_all[:].rearrange("p (m k h) -> p h m k", k=NB, h=2)
            r_to = rP[:].rearrange("p (m h k) -> p h m k", k=NB, h=2)
            for h in range(2):
                dve.tensor_copy(r_to[:, h], r_from[:, h]).then_inc(r_perm, 1)
            dve.wait_ge(rT_sb, (B + 3) // 4)
            for e in range(3):
                dve.tensor_copy(rS[0:R, e, :], rT[0:R, :]).then_inc(r_split, 1)
                dve.wait_ge(r_split, e + 1)
                if e < 2:
                    chain(dve.tensor_tensor(rT[0:R, :], rT[0:R, :], rS[0:R, e, :], ALU.subtract))

            dve.wait_ge(gram_ps, B * NC)
            dve.tensor_scalar(cov[:], gram[:, 0:C + 1], 1.0 / TOK, None, ALU.mult).then_inc(bn_c, 1)
            dve.wait_ge(bn_ps, 1)
            chain(dve.tensor_tensor(tmp[:], bank[1][:, 0:C], W_in[:], ALU.mult))
            chain(dve.tensor_reduce(small[:, 6:7], tmp[:], AX, ALU.add))
            chain(dve.tensor_copy(small[:, 7:8], bank[1][:, C:C + 1]))
            chain(dve.tensor_tensor(small[:, 8:9], small[:, 7:8], small[:, 7:8], ALU.mult))
            dve.tensor_tensor(small[:, 9:10], small[:, 6:7], small[:, 8:9], ALU.subtract).then_inc(bn_var, 1)
            dve.wait_ge(bn_rstd, 1)
            chain(dve.tensor_tensor(small[:, 11:12], small[:, 10:11], cols_in[:, 0:1], ALU.mult))
            chain(dve.tensor_scalar(Wz[:], W_in[:], small[:, 11:12], None, ALU.mult))
            chain(dve.tensor_reduce(small[:, 14:15], Wz[:], AX, ALU.add))
            chain(dve.tensor_scalar(small[:, 15:16], small[:, 14:15], 1.0 / C, None, ALU.mult))
            dve.tensor_scalar(Wz[:], Wz[:], small[:, 15:16], None, ALU.subtract).then_inc(bn_w, 1)
            chain(dve.tensor_tensor(small[:, 12:13], small[:, 7:8], small[:, 11:12], ALU.mult))
            chain(dve.tensor_tensor(zbias[:], cols_in[:, 1:2], small[:, 12:13], ALU.subtract))
            dve.wait_ge(bn_wps, 1)
            dve.tensor_copy(WzT[:], bank[2][:, 0:C]).then_inc(bn_done, 1)
            scan_vector(dve)

_INS = ["x", "L0_conv_w_qkv", "L0_conv_w_out", "L0_conv_g", "L0_conv_b_out", "L0_ffn_W", "L0_ffn_V", "L0_ffn_gamma", "L0_ffn_beta"]


def program(nc, shapes):
    t = {n: nc.dram_tensor(f"in_{n}", s, F32, kind="ExternalInput").ap() for n, s in shapes.items()}
    out = nc.dram_tensor("out", shapes["x"], F32, kind="ExternalOutput").ap()
    build(nc, t["x"].rearrange("b c h w -> b c (h w)"), t["L0_conv_w_qkv"], t["L0_conv_w_out"], t["L0_conv_b_out"],
          t["L0_conv_g"], t["L0_ffn_W"], t["L0_ffn_V"], t["L0_ffn_gamma"], t["L0_ffn_beta"],
          out.rearrange("b c h w -> b c (h w)"))


def kernel(**inputs):
    import concourse.bacc as bacc
    from concourse.bass_utils import run_bass_kernel_spmd

    nc = bacc.Bacc("TRN2", target_bir_lowering=False, num_devices=1)
    arrays = {n: np.ascontiguousarray(inputs[n]) for n in _INS}
    program(nc, {n: arrays[n].shape for n in _INS})
    r = run_bass_kernel_spmd(nc, [{f"in_{n}": arrays[n] for n in _INS}], core_ids=[0])
    return r.results[0]["out"]
```
